# Optimizing a Trainium2 kernel written in Bass

```python
import numpy as np
import jax
import jax.numpy as jnp

def _softmax(x, axis=-1):
    return jax.nn.softmax(x, axis=axis)

def _gelu(x):
    return jax.nn.gelu(x, approximate=True)

def _silu(x):
    return jax.nn.silu(x)

def _sigmoid(x):
    return jax.nn.sigmoid(x)

def _layernorm(x, axis=-1, eps=1e-05):
    m = jnp.mean(x, axis=axis, keepdims=True)
    v = jnp.var(x, axis=axis, keepdims=True)
    return (x - m) / jnp.sqrt(v + eps)

def _scatter_add(tgt, idx, src, axis=0):
    return tgt.at[idx].add(src)

def _segment_sum(src, seg, n):
    return jax.ops.segment_sum(src, seg, n)
kernel_name = 'mk_gnn_preln_d2_gnn_r8_c069a6'

def setup_inputs(seed: int=0):
    np.random.seed(seed)
    _w = jnp.asarray

    def _rec_inputs():
        import jax
        import jax.numpy as jnp
        _gk = jax.random.key(seed)
        x = -0.003407 + 1.001 * jax.random.normal(jax.random.fold_in(_gk, 1), (6250, 256), jnp.float32)
        _s = jax.random.randint(jax.random.fold_in(_gk, 2), (50000,), 0, 6250, jnp.int32)
        _d = jax.random.randint(jax.random.fold_in(_gk, 3), (50000,), 0, 6250, jnp.int32)
        _loop = jnp.arange(6250, dtype=jnp.int32)
        src = jnp.concatenate([_s, _d, _loop])
        dst = jnp.concatenate([_d, _s, _loop])
        _o = jnp.argsort(dst, stable=True)
        src = src[_o]
        dst = dst[_o]
        edge_attr_4 = 0.00117183 + 1.0004 * jax.random.normal(jax.random.fold_in(_gk, 12), (106250, 4), jnp.float32)
        edge_attr_8 = -0.000615933 + 0.999959 * jax.random.normal(jax.random.fold_in(_gk, 13), (106250, 8), jnp.float32)
        edge_weight1 = jax.random.uniform(jax.random.fold_in(_gk, 15), (106250, 1), jnp.float32, 0.0, 1)
        node_vec1 = jax.random.uniform(jax.random.fold_in(_gk, 16), (6250, 1), jnp.float32, 0.0, 1)
        return (x, src, dst, edge_attr_4, edge_attr_8, edge_weight1, node_vec1)
    x, src, dst, edge_attr_4, edge_attr_8, edge_weight1, node_vec1 = _rec_inputs()

    def _L0_gnn_setup():
        import jax, jax.numpy as jnp
        import numpy as np
        BS = 512
        EMBED = 256
        NHEAD = 8
        HDIM = EMBED // NHEAD
        E = BS * BS

        def _xavier(key, shape):
            lim = float(np.sqrt(6.0 / (shape[0] + shape[1])))
            return jax.random.uniform(key, shape, jnp.float32, -lim, lim)
        key = jax.random.key(seed)
        ks = jax.random.split(key, 6)
        feats = jax.random.normal(ks[0], (BS, EMBED), jnp.float32)
        dst = jnp.repeat(jnp.arange(BS), BS)
        src = jnp.tile(jnp.arange(BS), BS)
        edge_index = jnp.stack([src, dst], axis=1).astype(jnp.int32)
        edge_attr = jnp.zeros((E, 1), jnp.float32)
        return {'feats': feats, 'edge_index': edge_index, 'edge_attr': edge_attr, 'Wq': _xavier(ks[1], (EMBED, EMBED)), 'bq': jnp.zeros((EMBED,), jnp.float32), 'Wk': _xavier(ks[2], (EMBED, EMBED)), 'bk': jnp.zeros((EMBED,), jnp.float32), 'Wv': _xavier(ks[3], (EMBED, EMBED)), 'bv': jnp.zeros((EMBED,), jnp.float32), 'Wo': _xavier(ks[4], (EMBED, EMBED)), 'bo': jnp.zeros((EMBED,), jnp.float32)}
    _L0_gnn_all = _L0_gnn_setup()
    _L0_gnn_in = {k: v for k, v in _L0_gnn_all.items() if k in ('Wq', 'bq', 'Wk', 'bk', 'Wv', 'bv', 'Wo', 'bo')}
    del _L0_gnn_all

    def _L1_gnn_setup():
        import jax, jax.numpy as jnp
        import numpy as np
        import math
        N = 3750
        E = 75000
        MUL = 64
        NES = 8
        FCN = 64
        NUM_NEIGHBORS = 20.0
        SILU_NORM = 1.679
        INV_SQRT3 = 1.0 / math.sqrt(3.0)

        def _split(x):
            return (x[:, :MUL], x[:, MUL:].reshape(-1, MUL, 3))
        key = jax.random.key(seed)
        ks = jax.random.split(key, 16)
        inp = {'node_input': jax.random.normal(ks[0], (N, 4 * MUL), jnp.float32), 'node_attr': jnp.ones((N, 1), jnp.float32), 'edge_src': jax.random.randint(ks[1], (E,), 0, N), 'edge_dst': jax.random.randint(ks[2], (E,), 0, N), 'edge_attr': jax.random.normal(ks[3], (E, 4), jnp.float32), 'edge_scalars': jax.random.normal(ks[4], (E, NES), jnp.float32), 'sc_w0': jax.random.normal(ks[5], (MUL, MUL), jnp.float32), 'sc_w1': jax.random.normal(ks[6], (MUL, MUL), jnp.float32), 'lin1_w0': jax.random.normal(ks[7], (MUL, MUL), jnp.float32), 'lin1_w1': jax.random.normal(ks[8], (MUL, MUL), jnp.float32), 'fc_w1': jax.random.normal(ks[9], (NES, FCN), jnp.float32), 'fc_w2': jax.random.normal(ks[10], (FCN, 4 * MUL), jnp.float32), 'lin2_w00': jax.random.normal(ks[11], (MUL, MUL), jnp.float32), 'lin2_w01': jax.random.normal(ks[12], (MUL, MUL), jnp.float32), 'lin2_w10': jax.random.normal(ks[13], (MUL, MUL), jnp.float32), 'lin2_w11': jax.random.normal(ks[14], (MUL, MUL), jnp.float32)}
        return inp
    _L1_gnn_all = _L1_gnn_setup()
    _L1_gnn_in = {k: v for k, v in _L1_gnn_all.items() if k in ('sc_w0', 'sc_w1', 'lin1_w0', 'lin1_w1', 'fc_w1', 'fc_w2', 'lin2_w00', 'lin2_w01', 'lin2_w10', 'lin2_w11')}
    del _L1_gnn_all
    return {'x': x, 'src': src, 'dst': dst, 'edge_attr_4': edge_attr_4, 'edge_attr_8': edge_attr_8, 'edge_weight1': edge_weight1, 'node_vec1': node_vec1, 'L0_gnn_Wq': _L0_gnn_in['Wq'], 'L0_gnn_bq': _L0_gnn_in['bq'], 'L0_gnn_Wk': _L0_gnn_in['Wk'], 'L0_gnn_bk': _L0_gnn_in['bk'], 'L0_gnn_Wv': _L0_gnn_in['Wv'], 'L0_gnn_bv': _L0_gnn_in['bv'], 'L0_gnn_Wo': _L0_gnn_in['Wo'], 'L0_gnn_bo': _L0_gnn_in['bo'], 'L1_gnn_sc_w0': _L1_gnn_in['sc_w0'], 'L1_gnn_sc_w1': _L1_gnn_in['sc_w1'], 'L1_gnn_lin1_w0': _L1_gnn_in['lin1_w0'], 'L1_gnn_lin1_w1': _L1_gnn_in['lin1_w1'], 'L1_gnn_fc_w1': _L1_gnn_in['fc_w1'], 'L1_gnn_fc_w2': _L1_gnn_in['fc_w2'], 'L1_gnn_lin2_w00': _L1_gnn_in['lin2_w00'], 'L1_gnn_lin2_w01': _L1_gnn_in['lin2_w01'], 'L1_gnn_lin2_w10': _L1_gnn_in['lin2_w10'], 'L1_gnn_lin2_w11': _L1_gnn_in['lin2_w11']}

def reference(x, src, dst, edge_attr_4, edge_attr_8, edge_weight1, node_vec1, L0_gnn_Wq, L0_gnn_bq, L0_gnn_Wk, L0_gnn_bk, L0_gnn_Wv, L0_gnn_bv, L0_gnn_Wo, L0_gnn_bo, L1_gnn_sc_w0, L1_gnn_sc_w1, L1_gnn_lin1_w0, L1_gnn_lin1_w1, L1_gnn_fc_w1, L1_gnn_fc_w2, L1_gnn_lin2_w00, L1_gnn_lin2_w01, L1_gnn_lin2_w10, L1_gnn_lin2_w11):
    import jax
    import jax.numpy as jnp

    def _L0_gnn_ref(feats, edge_index, edge_attr, Wq, bq, Wk, bk, Wv, bv, Wo, bo):
        import jax, jax.numpy as jnp
        import numpy as np
        BS = 512
        EMBED = 256
        NHEAD = 8
        HDIM = EMBED // NHEAD
        E = BS * BS

        def _xavier(key, shape):
            lim = float(np.sqrt(6.0 / (shape[0] + shape[1])))
            return jax.random.uniform(key, shape, jnp.float32, -lim, lim)
        bs = feats.shape[0]
        scale = 1.0 / np.sqrt(HDIM)
        q = (feats @ Wq.T + bq).reshape(bs, NHEAD, HDIM).transpose(1, 0, 2)
        k = (feats @ Wk.T + bk).reshape(bs, NHEAD, HDIM).transpose(1, 0, 2)
        v = (feats @ Wv.T + bv).reshape(bs, NHEAD, HDIM).transpose(1, 0, 2)
        r, c = (edge_index[:, 0], edge_index[:, 1])
        qe = q[:, c, :]
        ke = k[:, r, :]
        ve = v[:, r, :]
        sim = jnp.einsum('hed,hed->eh', qe, ke) * scale
        m = jax.ops.segment_max(sim, c, num_segments=bs)
        p = jnp.exp(sim - m[c])
        s = jax.ops.segment_sum(p, c, num_segments=bs)
        attn = p / s[c]
        out_e = attn.T[..., None] * ve
        out_e = out_e.transpose(1, 0, 2).reshape(-1, NHEAD * HDIM)
        agg = jax.ops.segment_sum(out_e, c, num_segments=bs)
        return agg @ Wo.T + bo

    def _L1_gnn_ref(node_input, node_attr, edge_src, edge_dst, edge_attr, edge_scalars, sc_w0, sc_w1, lin1_w0, lin1_w1, fc_w1, fc_w2, lin2_w00, lin2_w01, lin2_w10, lin2_w11):
        import jax, jax.numpy as jnp
        import numpy as np
        import math
        N = 3750
        E = 75000
        MUL = 64
        NES = 8
        FCN = 64
        NUM_NEIGHBORS = 20.0
        SILU_NORM = 1.679
        INV_SQRT3 = 1.0 / math.sqrt(3.0)

        def _split(x):
            return (x[:, :MUL], x[:, MUL:].reshape(-1, MUL, 3))
        n = node_input.shape[0]
        inv_mul = 1.0 / math.sqrt(MUL)
        x0, x1 = _split(node_input)
        a = node_attr
        s0 = x0 @ sc_w0 * a * inv_mul
        s1 = jnp.einsum('nuc,uv->nvc', x1, sc_w1) * a[:, :, None] * inv_mul
        y0 = x0 @ lin1_w0 * a * inv_mul
        y1 = jnp.einsum('nuc,uv->nvc', x1, lin1_w1) * a[:, :, None] * inv_mul
        h = jax.nn.silu(edge_scalars @ fc_w1 * (1.0 / math.sqrt(NES))) * SILU_NORM
        w = h @ fc_w2 * (1.0 / math.sqrt(FCN))
        w_a, w_b, w_c, w_d = (w[:, :MUL], w[:, MUL:2 * MUL], w[:, 2 * MUL:3 * MUL], w[:, 3 * MUL:])
        xg0 = y0[edge_src]
        xg1 = y1[edge_src]
        ea0 = edge_attr[:, :1]
        ea1 = edge_attr[:, 1:4]
        mid0 = w_a * xg0 * ea0
        mid1 = w_b * jnp.einsum('euc,ec->eu', xg1, ea1) * INV_SQRT3
        mid2 = (w_c * xg0)[:, :, None] * ea1[:, None, :]
        mid3 = (w_d * ea0)[:, :, None] * xg1
        mids = jnp.concatenate([mid0, mid1, mid2.reshape(-1, 3 * MUL), mid3.reshape(-1, 3 * MUL)], axis=1)
        agg = jax.ops.segment_sum(mids, edge_dst, num_segments=n)
        agg = agg * (1.0 / math.sqrt(NUM_NEIGHBORS))
        z0a = agg[:, :MUL]
        z0b = agg[:, MUL:2 * MUL]
        z1a = agg[:, 2 * MUL:5 * MUL].reshape(n, MUL, 3)
        z1b = agg[:, 5 * MUL:].reshape(n, MUL, 3)
        inv2 = 1.0 / math.sqrt(2 * MUL)
        o0 = (z0a @ lin2_w00 + z0b @ lin2_w01) * a * inv2
        o1 = (jnp.einsum('nuc,uv->nvc', z1a, lin2_w10) + jnp.einsum('nuc,uv->nvc', z1b, lin2_w11)) * a[:, :, None] * inv2
        c_s = math.sin(math.pi / 8.0)
        c_x = math.cos(math.pi / 8.0)
        out0 = c_s * s0 + c_x * o0
        out1 = c_s * s1 + c_x * o1
        return jnp.concatenate([out0, out1.reshape(n, 3 * MUL)], axis=1)
    edge_index_t = jnp.stack([src, dst], axis=1)
    h = jnp.maximum(_layernorm(x, axis=-1), 0.0)
    x = x + _L0_gnn_ref(h, edge_index_t, edge_weight1, L0_gnn_Wq, L0_gnn_bq, L0_gnn_Wk, L0_gnn_bk, L0_gnn_Wv, L0_gnn_bv, L0_gnn_Wo, L0_gnn_bo)
    h = jnp.maximum(_layernorm(x, axis=-1), 0.0)
    x = x + _L1_gnn_ref(h, node_vec1, src, dst, edge_attr_4, edge_attr_8, L1_gnn_sc_w0, L1_gnn_sc_w1, L1_gnn_lin1_w0, L1_gnn_lin1_w1, L1_gnn_fc_w1, L1_gnn_fc_w2, L1_gnn_lin2_w00, L1_gnn_lin2_w01, L1_gnn_lin2_w10, L1_gnn_lin2_w11)
    return x

_drawn_inputs = setup_inputs


def setup_inputs(seed=0):
    import zlib

    import numpy as np

    out = dict(_drawn_inputs(seed))
    spreads = {'L0_gnn_bq': (0.0, 0.8),
     'L0_gnn_bk': (0.0, 0.8),
     'L0_gnn_bv': (0.0, 0.1),
     'L0_gnn_bo': (0.0, 0.1)}
    factors = {}
    for name, (base, spread) in spreads.items():
        noise = np.random.default_rng([zlib.crc32(name.encode()), seed]).standard_normal(out[name].shape)
        drawn = base * np.exp(spread * noise) if base else spread * noise
        out[name] = jnp.asarray(drawn.astype(out[name].dtype))
    for name, factor in factors.items():
        out[name] = (out[name] * factor).astype(out[name].dtype)
    return out
```

```python
import math
from contextlib import ExitStack

import concourse.bass as bass
from concourse import mybir

F32 = mybir.dt.float32
BF16 = mybir.dt.bfloat16
I32 = mybir.dt.int32
U32 = mybir.dt.uint32
ALU = mybir.AluOpType
ACT = mybir.ActivationFunctionType
AX_X = mybir.AxisListType.X

P = 128
N_NODES = 6250
N_EDGES = 106250
EMBED = 256
HEADS = 8
HDIM = EMBED // HEADS
MUL = 64
SCALARS = 8
EPS = 1e-5
TILES = 8
CHUNK = TILES * P
CHUNKS = -(-N_EDGES // CHUNK)
EDGE_TILES = CHUNKS * TILES
E_PAD = CHUNKS * CHUNK
NODE_TILES = 2 * (-(-(N_NODES + P) // (2 * P)))
N_PAD = NODE_TILES * P
HALF = TILES // 2
ROWS = 88
AGG0 = 3
MSG = HEADS + EMBED
AGG1 = 5
BLOCK_AT = (0, P, EMBED, EMBED + P, EMBED + P + MUL)
NEG = -1e30
UNROLL = 4


def build(nc, a):
    with ExitStack() as whole:
        s_turn = [whole.enter_context(nc.semaphore(f"s_turn_{e}")) for e in ("pool", "pe")]
        kv_table = nc.dram_tensor("kv_table", [N_PAD, 2 * EMBED], F32).ap()
        q_table = nc.dram_tensor("q_table", [N_PAD, EMBED], F32).ap()
        y_table = nc.dram_tensor("y_table", [N_PAD, EMBED], F32).ap()
        skip_table = nc.dram_tensor("skip_table", [N_PAD, EMBED], F32).ap()
        dst_rows = nc.dram_tensor("dst_rows", [CHUNKS, CHUNK // 2], F32).ap()
        new_rows = nc.dram_tensor("new_rows", [CHUNKS, CHUNK], F32).ap()
        s_io = whole.enter_context(nc.semaphore("s_io"))
        K = Constants(nc, whole)
        K.turn_pe = s_turn[1]
        load_constants(nc, a, K, dst_rows, new_rows)
        nodes_before_attention(nc, a, K, kv_table, q_table)
        with ExitStack() as one:
            acc = one.enter_context(nc.sbuf_tensor("attn_sum", [ROWS, AGG0, N_PAD], F32))
            attention_edges(nc, a, K, acc, kv_table, q_table, dst_rows, new_rows, s_turn, 4, 64, 4)
            nodes_between(nc, a, K, acc, y_table, skip_table)
        with ExitStack() as two:
            acc = two.enter_context(nc.sbuf_tensor("conv_sum", [P, AGG1, N_PAD], F32))
            convolution_edges(nc, a, K, acc, y_table, s_turn, 4, 64)
            nodes_after(nc, a, K, acc, skip_table)


class Constants:

    def __init__(self, nc, ctx):
        def sb(name, shape, dt=F32):
            return ctx.enter_context(nc.sbuf_tensor(name, shape, dt))

        self.ident = sb("ident", [P, P])
        self.iota = sb("iota", [P, P])
        self.place = sb("place", [HEADS, AGG0, ROWS])
        self.dst_rel = sb("dst_rel", [P, EDGE_TILES])
        self.part = sb("part", [P, 1])
        self.first = sb("first", [1, EDGE_TILES // 4], I32)


class Count:

    def __init__(self, eng, sem):
        self.eng, self.sem, self.n = eng, sem, 0

    def __call__(self, ins):
        self.n += 1
        ins.then_inc(self.sem, 1)
        self.eng.wait_ge(self.sem, self.n)


def wait_then(eng, sem, value, turn):
    eng.wait_ge(sem, value)
    eng.sem_inc(turn, 1)


def load_constants(nc, a, K, dst_rows, new_rows):
    GROUPS = EDGE_TILES // 4
    with ExitStack() as ctx:
        def sb(name, shape, dt=F32):
            return ctx.enter_context(nc.sbuf_tensor(name, shape, dt))

        dst_t = sb("dst_t", [P, EDGE_TILES], I32)
        first_t = sb("first_t", [P, GROUPS], I32)
        first_f = sb("first_f", [P, GROUPS])
        lin_i = sb("lin_i", [CHUNKS, CHUNK + 1], I32)
        lin = sb("lin", [CHUNKS, CHUNK + 1])
        rel = sb("rel", [CHUNKS, CHUNK], BF16)
        new = sb("new_line", [CHUNKS, CHUNK])
        s_in = ctx.enter_context(nc.semaphore("s_in"))
        s_v = ctx.enter_context(nc.semaphore("s_prep"))
        s_out = ctx.enter_context(nc.semaphore("s_prep_out"))
        block = ctx.enter_context(nc.Block())

        @block.sync
        def _(sp):
            for dst, src in ((dst_t[:, :], a["dst_tile"]), (first_t[:, :], a["first"].to_broadcast([P, GROUPS])),
                             (lin_i[:, :], a["dst_line"]), (K.ident[:, :], a["ident"]),
                             (K.iota[:, :], a["iota"].to_broadcast([P, P])), (K.place[:, :, :], a["place"]),
                             (K.first[:, :], a["first"]), (K.part[:, :], a["part"])):
                sp.dma_start(dst, src).then_inc(s_in, 16)
            sp.wait_ge(s_v, 6)
            sp.dma_start(dst_rows, rel[:, :].bitcast(F32)).then_inc(s_out, 16)
            sp.dma_start(new_rows, new[:, :]).then_inc(s_out, 16)
            sp.wait_ge(s_out, 32)

        @block.vector
        def _(v):
            step = Count(v, s_v)
            v.wait_ge(s_in, 16 * 8)
            step(v.tensor_copy(first_f[:, :], first_t[:, :]))
            step(v.tensor_copy(lin[:, :], lin_i[:, :]))
            step(v.tensor_tensor(K.dst_rel[:, :].rearrange("p (g t) -> p g t", t=4),
                                 dst_t[:, :].rearrange("p (g t) -> p g t", t=4),
                                 first_f[:, :].unsqueeze(2).to_broadcast([P, GROUPS, 4]), ALU.subtract))
            step(v.tensor_scalar(rel[:, :], lin[:, 1:CHUNK + 1], lin[:, 1:2], None, ALU.subtract))
            step(v.tensor_tensor(new[:, :], lin[:, 1:CHUNK + 1], lin[:, 0:CHUNK], ALU.not_equal))
            step(v.tensor_scalar(new[:, :], new[:, :], NEG, None, ALU.mult))


def layer_stats(v, stats, mean, rstd, tmp, step):
    cnt = EMBED
    me, mo = stats[:, :, 1], stats[:, :, 4]
    step(v.tensor_tensor(mean[:, :], me, mo, ALU.add))
    step(v.tensor_scalar(mean[:, :], mean[:, :], 0.5, None, ALU.mult))
    step(v.tensor_tensor(tmp[:, :], me, mo, ALU.subtract))
    step(v.tensor_tensor(tmp[:, :], tmp[:, :], tmp[:, :], ALU.mult))
    step(v.tensor_tensor(rstd[:, :], stats[:, :, 2], stats[:, :, 5], ALU.add))
    step(v.tensor_scalar(rstd[:, :], rstd[:, :], 1.0 / cnt, EPS, ALU.mult, ALU.add))
    step(v.scalar_tensor_tensor(out=rstd[:, :], in0=tmp[:, :], scalar=0.25, in1=rstd[:, :],
                                op0=ALU.mult, op1=ALU.add))



class NodePass:

    def __init__(self, nc, ctx, name, K, x_sb, w_sb, width):
        def sb(n, shape):
            return ctx.enter_context(nc.sbuf_tensor(f"{name}_{n}", shape, F32))

        def sem(n):
            return ctx.enter_context(nc.semaphore(f"{name}_{n}"))

        self.K, self.x_sb, self.w_sb, self.width = K, x_sb, w_sb, width
        self.h = sb("h", [P, 2, EMBED])
        self.hT = sb("hT", [P, 2, 2, P])
        self.stats = sb("stats", [P, NODE_TILES, 6])
        self.shift, self.scale, self.tmp = (sb(n, [P, NODE_TILES]) for n in ("shift", "scale", "tmp"))
        self.ps_t = [ctx.enter_context(nc.psum_tensor(f"{name}_turned{i}", [P, 2, P], F32)) for i in range(2)]
        self.ps_m = [ctx.enter_context(nc.psum_tensor(f"{name}_prod{i}", [P, 512 * -(-width // 512)], F32))
                     for i in range(2)]
        self.s_step, self.s_var, self.s_root, self.s_norm = sem("step"), sem("var"), sem("root"), sem("norm")
        self.s_stat, self.s_h, self.s_turned, self.s_copied = (
            sem(n) for n in ("s_stat", "s_h", "s_turned", "s_copied"))
        self.s_prod = [sem(f"s_prod{i}") for i in range(2)]
        self.s_taken = [sem(f"s_taken{i}") for i in range(2)]

    def statistics(self, v, step):
        with v.Fori(0, NODE_TILES) as i:
            v.bn_stats(self.stats[:, bass.ds(i, 1), :].rearrange("p a s -> p (a s)"),
                       self.x_sb[:, bass.ds(i, 1), :].rearrange("p a s -> p (a s)")).then_inc(self.s_stat, 1)
        v.wait_ge(self.s_stat, NODE_TILES)
        layer_stats(v, self.stats, self.shift, self.scale, self.tmp, step)
        v.sem_inc(self.s_var, 1)
        v.wait_ge(self.s_root, 1)
        step(v.reciprocal(self.scale[:, :], self.scale[:, :]))
        step(v.scalar_tensor_tensor(out=self.shift[:, :], in0=self.shift[:, :], scalar=-1.0,
                                    in1=self.scale[:, :], op0=ALU.mult, op1=ALU.mult))
        v.sem_inc(self.s_norm, 1)

    def scalar(self, act):
        act.wait_ge(self.s_var, 1)
        act.activation(self.scale[:, :], self.scale[:, :], ACT.Sqrt).then_inc(self.s_root, 1)
        act.wait_ge(self.s_norm, 1)

        def relu(j, s):
            act.activation(self.h[:, s, :], self.x_sb[:, bass.ds(j, 1), :].rearrange("p a f -> p (a f)"),
                           ACT.Relu, bias=self.shift[:, bass.ds(j, 1)],
                           scale=self.scale[:, bass.ds(j, 1)]).then_inc(self.s_h, 1)

        def copy(j, s, rounds):
            act.wait_ge(self.s_turned, j + 1)
            act.wait_ge(self.s_prod[s], rounds)
            act.activation(self.hT[:, s, :, :], self.ps_t[s][:, :, :], ACT.Copy).then_inc(self.s_copied, 1)

        relu(0, 0)
        with act.Fori(0, NODE_TILES // 2 - 1) as i:
            for s in range(2):
                act.wait_ge(self.s_turned, 2 * i + s)
                relu(2 * i + s + 1, 1 - s)
                copy(2 * i + s, s, i)
        last = NODE_TILES - 2
        act.wait_ge(self.s_turned, last)
        relu(last + 1, 1)
        copy(last, 0, last // 2)
        copy(last + 1, 1, last // 2)

    def tensor(self, pe):
        def turn(j, s):
            pe.wait_ge(self.s_h, j + 1)
            for c in range(2):
                mm = pe.transpose(self.ps_t[s][:, c, :], self.h[:, s, c * P:(c + 1) * P], self.K.ident[:, :])
            mm.then_inc(self.s_turned, 1)

        def project(j, s, rounds):
            pe.wait_ge(self.s_copied, j + 1)
            pe.wait_ge(self.s_taken[s], rounds)
            for n in range(0, self.width, 512):
                m = min(self.width, n + 512)
                for c in range(2):
                    mm = pe.matmul(self.ps_m[s][:, n:m], self.hT[:, s, c, :], self.w_sb[:, c, n:m],
                                   start=c == 0, stop=c == 1)
            mm.then_inc(self.s_prod[s], 1)

        turn(0, 0)
        with pe.Fori(0, NODE_TILES // 2 - 1) as i:
            for s in range(2):
                turn(2 * i + s + 1, 1 - s)
                project(2 * i + s, s, i)
        last = NODE_TILES - 2
        turn(last + 1, 1)
        project(last, 0, last // 2)
        project(last + 1, 1, last // 2)


def nodes_before_attention(nc, a, K, kv_table, q_table):
    WID = 3 * EMBED
    with ExitStack() as ctx:
        def sb(name, shape, dt=F32):
            return ctx.enter_context(nc.sbuf_tensor(name, shape, dt))

        def sem(name):
            return ctx.enter_context(nc.semaphore(name))

        x_sb = sb("x_sb", [P, NODE_TILES, EMBED])
        w_sb = sb("w_sb", [P, 2, WID])
        b_sb = sb("b_sb", [P, WID])
        o_sb = sb("o_sb", [P, 2, WID])
        N = NodePass(nc, ctx, "pre", K, x_sb, w_sb, WID)
        s_x, s_w, s_scaled = sem("s_x"), sem("s_w"), sem("s_scaled")
        s_stored = [sem(f"s_stored{i}") for i in range(2)]
        block = ctx.enter_context(nc.Block())
        x_d = a["x"].rearrange("(i p) f -> p i f", p=P)
        h = NODE_TILES // 2

        @block.sync
        def _(sp):
            sp.dma_start(x_sb[:, 0:h, :], x_d[:, 0:h, :]).then_inc(s_x, 16)
            sp.dma_start(x_sb[:, h:NODE_TILES, :], x_d[:, h:NODE_TILES, :]).then_inc(s_x, 16)
            sp.dma_start(w_sb[:, :, :], a["wqkv"]).then_inc(s_w, 16)
            sp.dma_start(b_sb[:, :], a["bqkv"].to_broadcast([P, WID])).then_inc(s_w, 16)
            with sp.Fori(0, h) as i:
                for s in range(2):
                    sp.wait_ge(N.s_taken[s], i + 1)
                    row = bass.ds((2 * i + s) * P, P)
                    sp.dma_start(kv_table[row, :], o_sb[:, s, 0:2 * EMBED]).then_inc(s_stored[s], 16)
                    sp.dma_start(q_table[row, :], o_sb[:, s, 2 * EMBED:WID]).then_inc(s_stored[s], 16)
            for s in range(2):
                sp.wait_ge(s_stored[s], 32 * h)

        @block.vector
        def _(v):
            step = Count(v, N.s_step)
            v.wait_ge(s_w, 32)
            step(v.tensor_scalar(w_sb[:, :, 2 * EMBED:WID], w_sb[:, :, 2 * EMBED:WID], HDIM ** -0.5, None, ALU.mult))
            step(v.tensor_scalar(b_sb[:, 2 * EMBED:WID], b_sb[:, 2 * EMBED:WID], HDIM ** -0.5, None, ALU.mult))
            v.sem_inc(s_scaled, 1)
            v.wait_ge(s_x, 32)
            N.statistics(v, step)
            with v.Fori(0, h) as i:
                for s in range(2):
                    v.wait_ge(N.s_prod[s], i + 1)
                    v.wait_ge(s_stored[s], 32 * i)
                    v.tensor_tensor(o_sb[:, s, :], N.ps_m[s][:, 0:WID], b_sb[:, :],
                                    ALU.add).then_inc(N.s_taken[s], 1)

        @block.scalar
        def _(act):
            N.scalar(act)

        @block.tensor
        def _(pe):
            pe.wait_ge(s_scaled, 1)
            N.tensor(pe)


def attention_edges(nc, a, K, acc, kv_table, q_table, dst_rows, new_rows, s_turn, per, W, R):
    GR = TILES // per
    turn_pool, turn_pe = s_turn
    with ExitStack() as ctx:
        def sb(name, shape, dt=F32):
            return ctx.enter_context(nc.sbuf_tensor(name, shape, dt))

        def sem(name):
            return ctx.enter_context(nc.semaphore(name))

        def psum(name, shape):
            return ctx.enter_context(nc.psum_tensor(name, shape, F32))

        kv = sb("kv", [P, R, TILES, 2 * EMBED])
        idx = sb("idx", [P, R, TILES], I32)
        rows = sb("rows", [P, 2, CHUNK], BF16)
        new = sb("new", [HEADS, 2, CHUNK])
        qw = sb("qw", [P, 2, EMBED])
        sel = sb("sel", [P, 2, TILES, W])
        selT = sb("selT", [P, CHUNK])
        prod = sb("prod", [P, 2, HALF, EMBED])
        score = sb("score", [P, 2, TILES * HEADS])
        top = sb("top", [HEADS, 2, CHUNK])
        diff = sb("diff", [P, TILES * HEADS])
        msg = sb("msg", [P, TILES, MSG])
        fall = sb("fall", [HEADS, 1])
        fade = sb("fade", [HEADS, 1])
        ps_q = [psum(f"ps_q{h}", [P, HALF, EMBED]) for h in range(2)]
        ps_s = psum("ps_s", [P, CHUNK])
        ps_a = [psum(f"ps_a{g}", [P, 512]) for g in range(2)]
        ps_top = ps_a[1][:, 448:512]
        ps_fade = ps_a[1][0:ROWS, 400:400 + AGG0]

        s_idx = [sem(f"s_idx{r}") for r in range(R)]
        s_kv = [sem(f"s_kv{r}") for r in range(R)]
        s_kv_used = [sem(f"s_kv_used{r}") for r in range(R)]
        s_rows = [sem(f"s_rows{u}") for u in range(2)]
        s_rows_used = [sem(f"s_rows_used{u}") for u in range(2)]
        s_new = [sem(f"s_new{u}") for u in range(2)]
        s_new_used = [sem(f"s_new_used{u}") for u in range(2)]
        (s_zero, s_selT, s_sel, s_q, s_mul, s_score, s_scoreT, s_run, s_top, s_diff, s_fall, s_fade,
         s_fadeR, s_exp, s_faded, s_msg, s_agg, s_sum) = (sem("s_" + n) for n in (
             "zero", "selT", "sel", "q", "mul", "score", "scoreT", "run", "top", "diff", "fall", "fade",
             "fadeR", "exp", "faded", "msg", "agg", "sum"))
        block = ctx.enter_context(nc.Block())
        U = UNROLL
        src_d = a["src_line"]

        @block.sync
        def _(sp):
            with sp.Fori(0, CHUNKS // U) as i:
                for m in range(U):
                    c, r, u, k = U * i + m, m % R, m % 2, i * (U // 2) + m // 2
                    n0 = sp.value_load(K.first[0:1, bass.ds(c * GR, 1)], min_val=0, max_val=N_NODES)
                    sp.wait_ge(s_kv[r], (i * (U // R) + m // R) * 16 * TILES)
                    sp.dma_start(idx[:, r, :], src_d[bass.ds(c, 1), :, :].rearrange("a p t -> p (a t)")
                                 ).then_inc(s_idx[r], 16)
                    sp.wait_ge(s_rows_used[u], k)
                    row = bass.ds(c, 1)
                    sp.dma_start(rows[:, u, :].bitcast(F32), dst_rows[row, :].to_broadcast([P, CHUNK // 2])).then_inc(s_rows[u], 16)
                    sp.dma_start(qw[:, u, :], q_table[bass.ds(n0, P), :]).then_inc(s_rows[u], 16)
                    sp.wait_ge(s_new_used[u], k)
                    sp.dma_start(new[:, u, :], new_rows[row, :].to_broadcast([HEADS, CHUNK])).then_inc(s_new[u], 16)

        @block.gpsimd
        def _(gp):
            with gp.Fori(0, CHUNKS // U) as i:
                for m in range(U):
                    r, k = m % R, i * (U // R) + m // R
                    wait_then(gp, s_idx[r], 16 * (k + 1), turn_pool)
                    wait_then(gp, s_kv_used[r], k, turn_pool)
                    for t in range(TILES):
                        gp.indirect_dma_start(kv[:, r, t, :], None, kv_table,
                                              bass.IndirectOffsetOnAxis(ap=idx[:, r, t:t + 1].bitcast(U32), axis=0)
                                              ).then_inc(s_kv[r], 16)

        @block.vector
        def _(v):
            v.memset(acc[:, :, :], 0.0).then_inc(s_zero, 1)
            v.memset(top[:, 1, CHUNK - 1:CHUNK], NEG).then_inc(s_zero, 1)
            v.wait_ge(s_zero, 2)

            def select_turned(c, u, k):
                v.wait_ge(s_rows[u], 32 * (k + 1))
                v.wait_ge(s_q, 2 * c)
                v.tensor_scalar(selT[:, :], rows[:, u, :], K.part[:, 0:1], None, ALU.is_equal).then_inc(s_selT, 1)

            def select(c, u):
                v.tensor_tensor(sel[:, u, :, :], K.iota[:, 0:W].unsqueeze(1).to_broadcast([P, TILES, W]),
                                K.dst_rel[:, bass.ds(c * TILES, TILES)].unsqueeze(2).to_broadcast([P, TILES, W]),
                                ALU.is_equal).then_inc(s_sel, 1)

            def scores(c, r, u, k):
                v.wait_ge(s_kv[r], 16 * TILES * (k + 1))
                for h in range(2):
                    v.wait_ge(s_q, 2 * c + h + 1)
                    v.tensor_tensor(prod[:, h, :, :], kv[:, r, h * HALF:(h + 1) * HALF, 0:EMBED],
                                    ps_q[h][:, :, :], ALU.mult).then_inc(s_mul, 1)
                for h in range(2):
                    v.wait_ge(s_mul, 2 * c + h + 1)
                    v.tensor_reduce(score[:, u, h * HALF * HEADS:(h + 1) * HALF * HEADS],
                                    prod[:, h, :, :].rearrange("p t (h d) -> p (t h) d", d=HDIM),
                                    AX_X, ALU.add).then_inc(s_score, 1)

            def weigh(c, u):
                v.wait_ge(s_fadeR, c + 1)
                v.wait_ge(s_exp, c)
                v.tensor_tensor(diff[:, :], score[:, u, :], ps_top, ALU.subtract).then_inc(s_diff, 1)

            def run(c, u, k):
                v.wait_ge(s_scoreT, c + 1)
                v.wait_ge(s_new[u], 16 * (k + 1))
                v.wait_ge(s_top, c)
                v.tensor_tensor_scan(top[:, u, :], new[:, u, :], ps_s[0:HEADS, :], top[:, 1 - u, CHUNK - 1:CHUNK],
                                     ALU.add, ALU.max).then_inc(s_run, 1)

            def spread(c, u):
                v.wait_ge(s_run, c + 1)
                v.tensor_tensor_scan(top[:, u, CHUNK - 2::-1], new[:, u, CHUNK - 1:0:-1], top[:, u, CHUNK - 2::-1],
                                     top[:, u, CHUNK - 1:CHUNK], ALU.add, ALU.max).then_inc(s_top, 1)
                v.wait_ge(s_top, c + 1)
                v.wait_ge(s_fade, c)
                v.tensor_scalar(fall[:, :], top[:, 1 - u, CHUNK - 1:CHUNK], top[:, u, 0:1], 0.0,
                                ALU.subtract, ALU.min).then_inc(s_fall, 1)
                v.sem_inc(s_new_used[u], 1)

            def messages(c, r):
                v.wait_ge(s_exp, c + 1)
                for h in range(2):
                    t = slice(h * HALF, (h + 1) * HALF)
                    ins = v.tensor_tensor(msg[:, t, HEADS:MSG].rearrange("p t (h d) -> p t h d", d=HDIM),
                                          kv[:, r, t, EMBED:2 * EMBED].rearrange("p t (h d) -> p t h d", d=HDIM),
                                          msg[:, t, 0:HEADS].unsqueeze(3).to_broadcast([P, HALF, HEADS, HDIM]),
                                          ALU.mult)
                    ins.then_inc(s_msg, 1)
                v.wait_ge(s_msg, 2 * c + 2)
                v.sem_inc(s_kv_used[r], 1)

            def first(c, g):
                return v.value_load(K.first[0:1, bass.ds(c * GR + g, 1)], min_val=0, max_val=N_NODES)

            def fade_sums(c):
                n0 = first(c, 0)
                v.wait_ge(s_sum, GR * c)
                v.tensor_tensor(acc[:, :, bass.ds(n0, 1)], acc[:, :, bass.ds(n0, 1)], ps_fade.unsqueeze(2),
                                ALU.mult).then_inc(s_faded, 1)
                v.wait_ge(s_faded, c + 1)

            def sums(c):
                for g in range(GR):
                    n0 = first(c, g)
                    v.wait_ge(s_agg, GR * c + g + 1)
                    v.wait_ge(s_sum, GR * c + g)
                    v.tensor_tensor(acc[:, :, bass.ds(n0, W)], acc[:, :, bass.ds(n0, W)],
                                    ps_a[g % 2][0:ROWS, 0:AGG0 * W].rearrange("p (k w) -> p k w", w=W),
                                    ALU.add).then_inc(s_sum, 1)

            def chunk(c, j, i):
                r, u, k = j % R, j % 2, i * (U // 2) + (j // 2)
                rk = i * (U // R) + j // R
                b, br, bu = (c - 1) if c is not None else CHUNKS - 1, (j - 1) % R, (j - 1) % 2
                first_one, last_one = isinstance(c, int) and c == 0, isinstance(c, int) and c == CHUNKS - 1
                if first_one:
                    select_turned(0, 0, 0)
                if c is not None and not last_one:
                    select_turned(c + 1, 1 - u, i * (U // 2) + (j + 1) // 2)
                if c is not None:
                    select(c, u)
                if not first_one:
                    weigh(b, bu)
                    fade_sums(b)
                if c is not None:
                    scores(c, r, u, rk)
                if not first_one:
                    messages(b, br)
                if c is not None:
                    run(c, u, k)
                    spread(c, u)
                if not first_one:
                    sums(b)

            walk(v, chunk)

        @block.scalar
        def _(act):
            def chunk(c, j, i):
                b = (c - 1) if c is not None else CHUNKS - 1
                if not isinstance(c, int) or c > 0:
                    act.wait_ge(s_diff, b + 1)
                    act.wait_ge(s_agg, GR * b)
                    act.activation(msg[:, :, 0:HEADS], diff[:, :].rearrange("p (t h) -> p t h", h=HEADS),
                                   ACT.Exp).then_inc(s_exp, 1)
                if c is not None:
                    act.wait_ge(s_fall, c + 1)
                    act.wait_ge(s_fadeR, c)
                    act.activation(fade[:, :], fall[:, :], ACT.Exp).then_inc(s_fade, 1)

            walk(act, chunk)

        @block.tensor
        def _(pe):
            def queries(c, u, k):
                pe.wait_ge(s_rows[u], 32 * (k + 1))
                for h in range(2):
                    pe.wait_ge(s_selT, c + 1)
                    if not isinstance(c, int) or c > 0:
                        pe.wait_ge(s_mul, 2 * c - 1 + h)
                    for t in range(h * HALF, (h + 1) * HALF):
                        mm = pe.matmul(ps_q[h][:, t - h * HALF, :], selT[:, t * P:(t + 1) * P],
                                       qw[:, u, :], start=True, stop=True)
                    mm.then_inc(s_q, 1)
                wait_then(pe, s_q, 2 * c + 2, turn_pe)
                pe.sem_inc(s_rows_used[u], 1)

            def chunk(c, j, i):
                u = j % 2
                if isinstance(c, int) and c == 0:
                    queries(0, 0, 0)
                if c is not None:
                    if not isinstance(c, int) or c < CHUNKS - 1:
                        queries(c + 1, 1 - u, i * (U // 2) + (j + 1) // 2)
                    pe.wait_ge(s_score, 2 * c + 2)
                    pe.wait_ge(s_run, c)
                    for t in range(TILES):
                        mm = pe.transpose(ps_s[0:HEADS, t * P:(t + 1) * P],
                                          score[:, u, t * HEADS:(t + 1) * HEADS], K.ident[:, :])
                    mm.then_inc(s_scoreT, 1)
                b, bu = (c - 1) if c is not None else CHUNKS - 1, (j - 1) % 2
                if not isinstance(c, int) or c > 0:
                    for g in range(GR):
                        pe.wait_ge(s_msg, 2 * b + (1 if (g + 1) * per <= HALF else 2))
                        pe.wait_ge(s_sum, GR * b + max(g - 1, 0))
                        if g == 1:
                            pe.wait_ge(s_faded, b + 1)
                        out = ps_a[g % 2][0:ROWS, 0:AGG0 * W].rearrange("p (k w) -> p k w", w=W)
                        for t in range(g * per, (g + 1) * per):
                            for m in range(AGG0):
                                mm = pe.matmul(out[:, m, :], msg[:, t, m * ROWS:(m + 1) * ROWS], sel[:, bu, t, :],
                                               start=t == g * per and m == 0, stop=t == (g + 1) * per - 1,
                                               skip_group_check=True)
                        mm.then_inc(s_agg, 1)
                if c is not None:
                    wait_then(pe, s_top, c + 1, turn_pe)
                    if not isinstance(c, int) or c > 0:
                        wait_then(pe, s_sum, GR * c, turn_pe)
                        wait_then(pe, s_diff, c, turn_pe)
                    for t in range(TILES):
                        mm = pe.transpose(ps_top[:, t * HEADS:(t + 1) * HEADS], top[:, u, t * P:(t + 1) * P],
                                          K.ident[0:HEADS, 0:HEADS])
                    wait_then(pe, s_fade, c + 1, turn_pe)
                    for m in range(AGG0):
                        mm = pe.matmul(ps_fade[:, m:m + 1], K.place[:, m, :], fade[:, :], start=True, stop=True)
                    mm.then_inc(s_fadeR, 1)

            walk(pe, chunk)


def walk(eng, chunk):
    chunk(0, 0, 0)
    with eng.Fori(0, CHUNKS // UNROLL - 1) as i:
        for j in range(1, UNROLL + 1):
            chunk(UNROLL * i + j, j, i)
    last = CHUNKS // UNROLL - 1
    for j in range(1, UNROLL):
        chunk(UNROLL * last + j, j, last)
    chunk(None, UNROLL, last)


def nodes_between(nc, a, K, acc, y_table, skip_table):
    WID = 2 * EMBED
    with ExitStack() as ctx:
        def sb(name, shape, dt=F32):
            return ctx.enter_context(nc.sbuf_tensor(name, shape, dt))

        def sem(name):
            return ctx.enter_context(nc.semaphore(name))

        x_sb = sb("x1_sb", [P, NODE_TILES, EMBED])
        w_sb = sb("w1_sb", [P, 2, WID])
        wo = sb("wo", [ROWS, AGG0, EMBED])
        bo = sb("bo", [P, EMBED])
        nv = sb("nv", [P, NODE_TILES])
        mean_v = sb("mean_v", [ROWS, 2, AGG0, P])
        y_sb = sb("y_sb", [P, 2, EMBED])
        N = NodePass(nc, ctx, "mid", K, x_sb, w_sb, WID)
        ps_r = N.ps_m
        ps_o = N.ps_t
        s_x, s_w, s_y, s_skip, s_scaled, s_recip = (
            sem(n) for n in ("m_x", "m_w", "m_y", "m_skip", "m_scaled", "m_recip"))
        s_spread, s_mean, s_out, s_added, s_res, s_bias = (
            sem(n) for n in ("m_spread", "m_mean", "m_out", "m_added", "m_res", "m_bias"))
        s_stored = [sem(f"m_stored{i}") for i in range(2)]
        block = ctx.enter_context(nc.Block())
        h = NODE_TILES // 2

        @block.sync
        def _(sp):
            sp.dma_start(x_sb[:, :, :], a["x"].rearrange("(i p) f -> p i f", p=P)).then_inc(s_x, 16)
            for dst, src in ((w_sb[:, :, :], a["wys"]), (wo[:, :, :], a["wo"]), (nv[:, :], a["nv"]),
                             (bo[:, :], a["bo"].to_broadcast([P, EMBED]))):
                sp.dma_start(dst, src).then_inc(s_w, 16)
            with sp.Fori(0, h) as i:
                for s in range(2):
                    sp.wait_ge(N.s_taken[s], i + 1)
                    sp.dma_start(y_table[bass.ds((2 * i + s) * P, P), :], y_sb[:, s, :]).then_inc(s_stored[s], 16)
                    sp.dma_start(skip_table[bass.ds((2 * i + s) * P, P), :],
                                 x_sb[:, bass.ds(2 * i + s, 1), :].rearrange("p a f -> p (a f)")
                                 ).then_inc(s_stored[s], 16)
            for s in range(2):
                sp.wait_ge(s_stored[s], 32 * h)

        @block.vector
        def _(v):
            step = Count(v, N.s_step)
            step(v.tensor_scalar(acc[0:HEADS, 0, :], acc[0:HEADS, 0, :], 1e-15, None, ALU.max))
            v.reciprocal(acc[0:HEADS, 0, :], acc[0:HEADS, 0, :]).then_inc(s_recip, 1)
            v.wait_ge(s_recip, 1)
            v.wait_ge(s_w, 64)
            step(v.tensor_scalar(w_sb[:, :, 0:EMBED], w_sb[:, :, 0:EMBED], MUL ** -0.5, None, ALU.mult))
            step(v.tensor_scalar(w_sb[:, :, EMBED:WID], w_sb[:, :, EMBED:WID],
                                 math.sin(math.pi / 8.0) * MUL ** -0.5, None, ALU.mult))
            v.sem_inc(s_scaled, 1)
            v.wait_ge(s_x, 16)

            def normalise(j, s):
                v.wait_ge(s_spread, j + 1)
                v.tensor_tensor(mean_v[:, s, :, :], acc[:, :, bass.ds(j * P, P)],
                                ps_r[s][0:ROWS, 0:AGG0 * P].rearrange("p (k n) -> p k n", n=P),
                                ALU.mult).then_inc(s_mean, 1)

            def add(j, s):
                row = x_sb[:, bass.ds(j, 1), :].rearrange("p a f -> p (a f)")
                v.wait_ge(s_out, j + 1)
                v.tensor_tensor(row, row, ps_o[s][:, :, :].rearrange("p a b -> p (a b)"), ALU.add).then_inc(s_added, 1)

            normalise(0, 0)
            with v.Fori(0, h - 1) as i:
                for s in range(2):
                    normalise(2 * i + s + 1, 1 - s)
                    add(2 * i + s, s)
            normalise(NODE_TILES - 1, 1)
            add(NODE_TILES - 2, 0)
            add(NODE_TILES - 1, 1)
            v.wait_ge(s_added, NODE_TILES)
            step(v.tensor_tensor(x_sb[:, :, :], x_sb[:, :, :],
                                 bo[:, :].unsqueeze(1).to_broadcast([P, NODE_TILES, EMBED]), ALU.add))
            N.statistics(v, step)
            with v.Fori(0, h) as i:
                for s in range(2):
                    j = 2 * i + s
                    row = x_sb[:, bass.ds(j, 1), :].rearrange("p a f -> p (a f)")
                    v.wait_ge(N.s_prod[s], i + 1)
                    v.wait_ge(s_stored[s], 32 * i)
                    v.tensor_scalar(y_sb[:, s, :], N.ps_m[s][:, 0:EMBED], nv[:, bass.ds(j, 1)], None,
                                    ALU.mult).then_inc(s_y, 1)
                    v.wait_ge(s_y, j + 1)
                    v.scalar_tensor_tensor(out=row, in0=N.ps_m[s][:, EMBED:WID], scalar=nv[:, bass.ds(j, 1)],
                                           in1=row, op0=ALU.mult, op1=ALU.add).then_inc(N.s_taken[s], 1)

        @block.scalar
        def _(act):
            N.scalar(act)

        @block.tensor
        def _(pe):
            pe.wait_ge(s_w, 64)
            pe.wait_ge(s_recip, 1)
            pe.wait_ge(s_scaled, 1)

            def spread(j, s):
                pe.sem_inc(K.turn_pe, 1)
                for k in range(AGG0):
                    mm = pe.matmul(ps_r[s][0:ROWS, k * P:(k + 1) * P], K.place[:, k, :],
                                   acc[0:HEADS, 0, bass.ds(j * P, P)], start=True, stop=True)
                mm.then_inc(s_spread, 1)

            def out(j, s):
                pe.wait_ge(s_mean, j + 1)
                for k in range(AGG0):
                    mm = pe.matmul(ps_o[s][:, :, :].rearrange("p a b -> p (a b)"), mean_v[:, s, k, :], wo[:, k, :],
                                   start=k == 0, stop=k == AGG0 - 1)
                mm.then_inc(s_out, 1)

            spread(0, 0)
            with pe.Fori(0, h - 1) as i:
                for s in range(2):
                    pe.wait_ge(s_added, 2 * i)
                    spread(2 * i + s + 1, 1 - s)
                    out(2 * i + s, s)
            pe.wait_ge(s_added, NODE_TILES - 2)
            spread(NODE_TILES - 1, 1)
            out(NODE_TILES - 2, 0)
            out(NODE_TILES - 1, 1)
            N.tensor(pe)


def convolution_edges(nc, a, K, acc, y_table, s_turn, per, W):
    GR = EDGE_TILES // per
    U = 4
    with ExitStack() as ctx:
        def sb(name, shape, dt=F32):
            return ctx.enter_context(nc.sbuf_tensor(name, shape, dt))

        def sem(name):
            return ctx.enter_context(nc.semaphore(name))

        def psum(name, shape):
            return ctx.enter_context(nc.psum_tensor(name, shape, F32))

        y = sb("y", [P, U, per, EMBED])
        idx = sb("idx1", [P, 2, TILES], I32)
        es = sb("es", [2 * SCALARS, U, 2 * P])
        ea = sb("ea", [P, EDGE_TILES, 4])
        fc1 = sb("fc1", [2 * SCALARS, P])
        fc2 = sb("fc2", [P, 2, EMBED])
        hid = sb("hid", [P, 2, 2 * P])
        w_ad = sb("w_ad", [P, 2, per, P])
        msg = sb("msg1", [P, 2, per, EMBED + 5 * MUL])
        sel = sb("sel1", [P, 2, per, W])
        sel_ax = sb("sel_ax", [P, 2, per, 3, W])
        ps_h = [psum(f"ps_h{u}", [P, 512]) for u in range(2)]
        ps_ad = [psum(f"ps_ad{u}", [P, per, P]) for u in range(2)]
        ps_cb = [psum(f"ps_cb{u}", [P, per, P]) for u in range(2)]
        ps_a = [psum(f"ps_c{u}", [P, 512]) for u in range(2)]
        s_idx = [sem(f"c_idx{r}") for r in range(2)]
        s_y = [sem(f"c_y{r}") for r in range(U)]
        s_es = [sem(f"c_es{r}") for r in range(U)]
        (s_in, s_zero, s_hid, s_silu, s_w, s_ad, s_sel, s_ax, s_msg, s_agg, s_prep) = (
            sem("c_" + n) for n in ("in", "zero", "hid", "silu", "w", "ad", "sel", "ax", "msg", "agg", "prep"))
        s_sum = [sem(f"c_sum{u}") for u in range(2)]
        block = ctx.enter_context(nc.Block())
        turn_pool, turn_pe = s_turn

        @block.sync
        def _(sp):
            for dst, src in ((ea[:, :, :], a["ea"]), (fc1[:, :], a["fc1"]), (fc2[:, :, :], a["fc2"])):
                sp.dma_start(dst, src).then_inc(s_in, 16)
            def load(i):
                for m in range(U):
                    r = m // 2
                    if m % 2 == 0:
                        for k in range(2):
                            sp.wait_ge(s_y[m + k], i * 16 * per)
                        sp.dma_start(idx[:, r, :],
                                     a["src_line"][bass.ds(2 * i + r, 1), :, :].rearrange("a p t -> p (a t)")
                                     ).then_inc(s_idx[r], 16)
                    if not isinstance(i, int):
                        sp.wait_ge(s_hid, U * i + m - U + 1)
                    sp.dma_start(es[:, m, :], a["es"][bass.ds(U * i + m, 1), :, :].rearrange("a k n -> k (a n)")
                                 ).then_inc(s_es[m], 16)

            load(0)
            with sp.Fori(1, GR // U) as i:
                load(i)

        @block.gpsimd
        def _(gp):
            def gather(i):
                for m in range(U):
                    if m % 2 == 0:
                        wait_then(gp, s_idx[m // 2], 16 * (i + 1), turn_pool)
                    if not isinstance(i, int):
                        wait_then(gp, s_msg, U * i + m - U + 1, turn_pool)
                    for t in range(per):
                        q = (m % 2) * per + t
                        gp.indirect_dma_start(y[:, m, t, :], None, y_table,
                                              bass.IndirectOffsetOnAxis(ap=idx[:, m // 2, q:q + 1].bitcast(U32), axis=0)
                                              ).then_inc(s_y[m], 16)

            gather(0)
            with gp.Fori(1, GR // U) as i:
                gather(i)

        @block.vector
        def _(v):
            step = Count(v, s_prep)
            v.memset(acc[:, :, :], 0.0).then_inc(s_zero, 1)
            v.wait_ge(s_in, 48)
            step(v.tensor_scalar(fc2[:, :, :], fc2[:, :, :], 1.679 * MUL ** -0.5, None, ALU.mult))
            v.wait_ge(s_zero, 1)

            def messages(g, r, i):
                u = r % 2
                v.tensor_tensor(sel[:, u, :, :], K.iota[:, 0:W].unsqueeze(1).to_broadcast([P, per, W]),
                                K.dst_rel[:, bass.ds(g * per, per)].unsqueeze(2).to_broadcast([P, per, W]),
                                ALU.is_equal).then_inc(s_sel, 1)
                v.wait_ge(s_sel, g + 1)
                v.tensor_tensor(sel_ax[:, u, :, :, :],
                                sel[:, u, :, :].unsqueeze(2).to_broadcast([P, per, 3, W]),
                                ea[:, bass.ds(g * per, per), 1:4].unsqueeze(3).to_broadcast([P, per, 3, W]),
                                ALU.mult).then_inc(s_ax, 1)
                v.wait_ge(s_y[r], 16 * per * (i + 1))
                v.wait_ge(s_w, g + 1)
                y0 = y[:, r, :, 0:MUL]
                y1 = y[:, r, :, MUL:EMBED].rearrange("p t (c f) -> p t c f", c=3)
                v.tensor_tensor(msg[:, u, :, EMBED + MUL:].rearrange("p t (c f) -> p t c f", f=MUL)[:, :, 0:3:2, :],
                                ps_cb[u][:, :, 0:MUL].unsqueeze(2).to_broadcast([P, per, 2, MUL]),
                                y0.unsqueeze(2).to_broadcast([P, per, 2, MUL]), ALU.mult)
                v.tensor_tensor(msg[:, u, :, EMBED:].rearrange("p t (c f) -> p t c f", f=MUL)[:, :, 0:5:2, :],
                                ps_cb[u][:, :, MUL:P].unsqueeze(2).to_broadcast([P, per, 3, MUL]), y1, ALU.mult)
                v.wait_ge(s_ad, g + 1)
                v.tensor_tensor(msg[:, u, :, 0:MUL], w_ad[:, u, :, 0:MUL], y0, ALU.mult)
                v.tensor_tensor(msg[:, u, :, MUL:EMBED].rearrange("p t (c f) -> p t c f", c=3),
                                w_ad[:, u, :, MUL:P].unsqueeze(2).to_broadcast([P, per, 3, MUL]), y1,
                                ALU.mult).then_inc(s_msg, 1)

            def sums(g, j, i):
                u = j % 2
                n0 = v.value_load(K.first[0:1, bass.ds(g, 1)], min_val=0, max_val=N_NODES)
                v.wait_ge(s_agg, g + 1)
                v.wait_ge(s_sum[1 - u], 2 * i + (j + 1) // 2)
                v.tensor_tensor(acc[:, :, bass.ds(n0, W)], acc[:, :, bass.ds(n0, W)],
                                ps_a[u][:, 0:AGG1 * W].rearrange("p (k w) -> p k w", w=W),
                                ALU.add).then_inc(s_sum[u], 1)

            def group(g, j, i):
                if g is not None:
                    messages(g, j % U, i + j // U)
                if not isinstance(g, int) or g > 0:
                    sums(g - 1 if g is not None else GR - 1, j - 1, i)

            walk_groups(v, group, GR)

        @block.scalar
        def _(act):
            def silu(g, u):
                act.wait_ge(s_hid, g + 1)
                act.activation(hid[:, u, :], ps_h[u][:, 0:2 * P], ACT.Silu, scale=SCALARS ** -0.5).then_inc(s_silu, 1)

            def group(g, j, i):
                if g is None:
                    return
                if not isinstance(g, int) or g < GR - 1:
                    silu(g + 1, (j + 1) % 2)
                act.wait_ge(s_w, g + 1)
                u = j % 2
                for t in range(per):
                    ins = act.activation(w_ad[:, u, t, :], ps_ad[u][:, t, :], ACT.Copy,
                                         scale=ea[:, bass.ds(g * per + t, 1), 0:1].rearrange("p a b -> p (a b)"))
                ins.then_inc(s_ad, 1)

            act.wait_ge(s_in, 48)
            silu(0, 0)
            walk_groups(act, group, GR)

        @block.tensor
        def _(pe):
            def hidden(g, r, i):
                wait_then(pe, s_es[r], 16 * (i + 1), turn_pe)
                pe.matmul(ps_h[r % 2][:, 0:2 * P], fc1[:, :], es[:, r, :], start=True, stop=True).then_inc(s_hid, 1)

            def group(g, j, i):
                u = j % 2
                if g is not None:
                    if not isinstance(g, int) or g < GR - 1:
                        hidden(g + 1, (j + 1) % U, i + (j + 1) // U)
                    pe.wait_ge(s_silu, g + 1)
                    if not isinstance(g, int) or g > 1:
                        pe.wait_ge(s_msg, g - 1)
                    for t in range(per):
                        for q, out in enumerate((ps_ad[u], ps_cb[u])):
                            mm = pe.matmul(out[:, t, :], hid[:, u, (t % 2) * P:(t % 2 + 1) * P],
                                           fc2[:, t // 2, q * P:(q + 1) * P], start=True, stop=True)
                    mm.then_inc(s_w, 1)
                if not isinstance(g, int) or g > 0:
                    b, bu = (g - 1) if g is not None else GR - 1, (j - 1) % 2
                    pe.wait_ge(s_msg, b + 1)
                    pe.wait_ge(s_sum[bu], 2 * i + (j - 1) // 2)
                    out = ps_a[bu][:, 0:AGG1 * W].rearrange("p (k w) -> p k w", w=W)
                    for t in range(per):
                        for m in range(AGG1):
                            at = BLOCK_AT[m]
                            mm = pe.matmul(out[:, m, :], msg[:, bu, t, at:at + P],
                                           sel[:, bu, t, :] if m < 2 else sel_ax[:, bu, t, m - 2, :], start=t == 0 and m == 0, stop=t == per - 1,
                                           skip_group_check=True)
                    mm.then_inc(s_agg, 1)

            pe.wait_ge(s_in, 48)
            pe.wait_ge(s_prep, 1)
            hidden(0, 0, 0)
            walk_groups(pe, group, GR)


def walk_groups(eng, group, n):
    group(0, 0, 0)
    with eng.Fori(0, n // 4 - 1) as i:
        for j in range(1, 5):
            group(4 * i + j, j, i)
    last = n // 4 - 1
    for j in range(1, 4):
        group(4 * last + j, j, last)
    group(None, 4, last)


def nodes_after(nc, a, K, acc, skip_table):
    with ExitStack() as ctx:
        def sb(name, shape, dt=F32):
            return ctx.enter_context(nc.sbuf_tensor(name, shape, dt))

        def sem(name):
            return ctx.enter_context(nc.semaphore(name))

        x_sb = sb("skip", [P, NODE_TILES, EMBED])
        w_sb = sb("w_fin", [P, AGG1, EMBED])
        nv = sb("nv_fin", [P, NODE_TILES])
        own = sb("own", [P, 2, AGG1, P])
        ps = [ctx.enter_context(nc.psum_tensor(f"ps_f{s}", [P, 512], F32)) for s in range(2)]
        s_x, s_w, s_scaled, s_own, s_fin, s_out = (sem("f_" + n) for n in ("x", "w", "scaled", "own", "fin", "out"))
        s_prod = [sem(f"f_prod{s}") for s in range(2)]
        block = ctx.enter_context(nc.Block())
        h = NODE_TILES // 2

        @block.sync
        def _(sp):
            sp.dma_start(w_sb[:, :, :], a["wfin"].rearrange("k p f -> p k f")).then_inc(s_w, 16)
            sp.dma_start(nv[:, :], a["nv"]).then_inc(s_w, 16)
            sp.dma_start(x_sb[:, :, :], skip_table.rearrange("(i p) f -> p i f", p=P)).then_inc(s_x, 16)
            with sp.Fori(0, h) as i:
                for s in range(2):
                    j = 2 * i + s
                    sp.wait_ge(s_fin, j + 1)
                    sp.dma_start(a["out"][bass.ds(j * P, P), :],
                                 x_sb[:, bass.ds(j, 1), :].rearrange("p a f -> p (a f)")).then_inc(s_out, 16)
            sp.wait_ge(s_out, 16 * NODE_TILES)

        @block.vector
        def _(v):
            scale = math.cos(math.pi / 8.0) / math.sqrt(2 * MUL) / math.sqrt(20.0)
            v.wait_ge(s_w, 32)
            v.tensor_scalar(w_sb[:, 0:2, :], w_sb[:, 0:2, :], scale, None, ALU.mult).then_inc(s_scaled, 1)
            for low, m, f in ((True, slice(2, 4), scale / math.sqrt(3.0)), (False, slice(2, 4), scale),
                              (True, slice(4, 5), scale), (False, slice(4, 5), scale / math.sqrt(3.0))):
                q = slice(0, MUL) if low else slice(MUL, P)
                v.tensor_scalar(w_sb[q, m, :], w_sb[q, m, :], f, None, ALU.mult).then_inc(s_scaled, 1)
            v.wait_ge(s_x, 16)
            with v.Fori(0, h) as i:
                for s in range(2):
                    j = 2 * i + s
                    row = x_sb[:, bass.ds(j, 1), :].rearrange("p a f -> p (a f)")
                    v.wait_ge(s_prod[s], i + 1)
                    v.scalar_tensor_tensor(out=row, in0=ps[s][:, 0:EMBED], scalar=nv[:, bass.ds(j, 1)], in1=row,
                                           op0=ALU.mult, op1=ALU.add).then_inc(s_fin, 1)

        @block.scalar
        def _(act):
            with act.Fori(0, h) as i:
                for s in range(2):
                    act.wait_ge(s_prod[s], i)
                    act.activation(own[:, s, :, :], acc[:, :, bass.ds((2 * i + s) * P, P)], ACT.Copy).then_inc(s_own, 1)

        @block.tensor
        def _(pe):
            pe.wait_ge(s_scaled, 5)
            with pe.Fori(0, h) as i:
                for s in range(2):
                    pe.wait_ge(s_own, 2 * i + s + 1)
                    pe.wait_ge(s_fin, 2 * i)
                    for k in range(AGG1):
                        mm = pe.matmul(ps[s][:, 0:EMBED], own[:, s, k, :], w_sb[:, k, :], start=k == 0, stop=k == AGG1 - 1)
                    mm.then_inc(s_prod[s], 1)


def kernel(**inputs):
    import numpy as np
    import concourse.bacc as bacc
    from concourse.bass_utils import run_bass_kernel_spmd

    d = {k: np.asarray(x) for k, x in inputs.items()}
    f = np.float32

    def rows(x, n, value=0):
        return np.concatenate([x, np.full((n - x.shape[0],) + x.shape[1:], value, x.dtype)])

    def by_tile(x):
        return np.ascontiguousarray(np.swapaxes(x.reshape(EDGE_TILES, P, *x.shape[1:]), 0, 1))

    src = rows(d["src"].astype(np.int32), E_PAD)
    dst = rows(d["dst"].astype(np.int32), E_PAD, N_NODES)
    ext = np.concatenate([np.full(1, -1, np.int32), dst])
    es = rows(d["edge_attr_8"], E_PAD).reshape(EDGE_TILES // 4, 2, 2, P, SCALARS)
    es = es.transpose(0, 1, 4, 2, 3).reshape(EDGE_TILES // 4, 2 * SCALARS, 2 * P)
    L0 = {n: d["L0_gnn_" + n] for n in ("Wq", "bq", "Wk", "bk", "Wv", "bv", "Wo", "bo")}
    L1 = {n: d["L1_gnn_" + n] for n in ("sc_w0", "sc_w1", "lin1_w0", "lin1_w1", "fc_w1", "fc_w2",
                                        "lin2_w00", "lin2_w01", "lin2_w10", "lin2_w11")}
    wqkv = np.concatenate([L0["Wk"].T, L0["Wv"].T, L0["Wq"].T], 1).reshape(2, P, 3 * EMBED).transpose(1, 0, 2)
    wo = np.concatenate([np.zeros((HEADS, EMBED), f), L0["Wo"].T]).reshape(AGG0, ROWS, EMBED).transpose(1, 0, 2)
    wys = np.zeros((EMBED, 2 * EMBED), f)
    wfin = np.zeros((AGG1, P, EMBED), f)
    wys[:MUL, :MUL] = L1["lin1_w0"]
    wys[:MUL, EMBED:EMBED + MUL] = L1["sc_w0"]
    wfin[0, :MUL, :MUL] = L1["lin2_w00"]
    for c in range(3):
        wys[MUL + c::3, MUL * (c + 1):MUL * (c + 2)] = L1["lin1_w1"]
        wys[MUL + c::3, EMBED + MUL + c::3] = L1["sc_w1"]
        wfin[(c + 1) // 2, ((c + 1) % 2) * MUL:((c + 1) % 2 + 1) * MUL, MUL + c::3] = L1["lin2_w11"]
        low, high = slice(0, MUL), slice(MUL, P)
        wfin[2 + c, low if c == 2 else high, MUL + c::3] = L1["lin2_w10"]
        wfin[2 + c, high if c == 2 else low, :MUL] = L1["lin2_w01"]
    wys = wys.reshape(2, P, 2 * EMBED).transpose(1, 0, 2)
    fc1 = np.zeros((2 * SCALARS, P), f)
    fc1[:SCALARS, :MUL] = fc1[SCALARS:, MUL:] = L1["fc_w1"]
    part = [L1["fc_w2"][:, MUL * k:MUL * (k + 1)] for k in (0, 3, 2, 1)]
    fc2 = np.zeros((P, 2, EMBED), f)
    fc2[:MUL, 0] = fc2[MUL:, 1] = np.concatenate(part, 1)
    place = np.zeros((HEADS, AGG0 * ROWS), f)
    for h in range(HEADS):
        place[h, h] = 1.0
        place[h, HEADS + h * HDIM:HEADS + (h + 1) * HDIM] = 1.0
    arrays = {
        "x": rows(d["x"], N_PAD),
        "src_line": src.reshape(CHUNKS, TILES, P).transpose(0, 2, 1),
        "dst_tile": by_tile(dst),
        "dst_line": np.lib.stride_tricks.sliding_window_view(ext, CHUNK + 1)[::CHUNK],
        "first": dst[None, ::4 * P],
        "ident": np.eye(P, dtype=f),
        "iota": np.arange(P, dtype=f)[None],
        "part": np.arange(P, dtype=f)[:, None],
        "place": place.reshape(HEADS, AGG0, ROWS),
        "wqkv": wqkv, "bqkv": np.concatenate([L0["bk"], L0["bv"], L0["bq"]])[None],
        "wo": wo, "bo": L0["bo"][None], "wys": wys, "wfin": wfin, "fc1": fc1, "fc2": fc2,
        "nv": rows(d["node_vec1"], N_PAD)[:, 0].reshape(NODE_TILES, P).T,
        "ea": by_tile(rows(d["edge_attr_4"], E_PAD)),
        "es": es,
    }
    nc = bacc.Bacc("TRN2", target_bir_lowering=False, num_devices=1)
    aps, feed = {}, {}
    for n, x in arrays.items():
        x = np.ascontiguousarray(x)
        feed["in_" + n] = x
        aps[n] = nc.dram_tensor("in_" + n, x.shape, mybir.dt.from_np(x.dtype), kind="ExternalInput").ap()
    aps["out"] = nc.dram_tensor("out", (N_PAD, EMBED), F32, kind="ExternalOutput").ap()
    build(nc, aps)
    r = run_bass_kernel_spmd(nc, [feed], core_ids=[0])
    return r.results[0]["out"][:N_NODES]
```

```python
import math
from contextlib import ExitStack

import concourse.bass as bass
from concourse import mybir

F32 = mybir.dt.float32
BF16 = mybir.dt.bfloat16
I32 = mybir.dt.int32
U32 = mybir.dt.uint32
ALU = mybir.AluOpType
ACT = mybir.ActivationFunctionType
AX_X = mybir.AxisListType.X

P = 128
N_NODES = 6250
N_EDGES = 106250
EMBED = 256
HEADS = 8
HDIM = EMBED // HEADS
MUL = 64
SCALARS = 8
EPS = 1e-5
TILES = 8
CHUNK = TILES * P
CHUNKS = -(-N_EDGES // CHUNK)
EDGE_TILES = CHUNKS * TILES
E_PAD = CHUNKS * CHUNK
NODE_TILES = 2 * (-(-(N_NODES + P) // (2 * P)))
N_PAD = NODE_TILES * P
HALF = TILES // 2
ROWS = 88
AGG0 = 3
MSG = HEADS + EMBED
AGG1 = 5
BLOCK_AT = (0, P, EMBED, EMBED + P, EMBED + P + MUL)
NEG = -1e30
UNROLL = 4


def build(nc, a):
    with ExitStack() as whole:
        s_turn = [whole.enter_context(nc.semaphore(f"s_turn_{e}")) for e in ("pool", "pe")]
        kv_table = nc.dram_tensor("kv_table", [N_PAD, 2 * EMBED], F32).ap()
        q_table = nc.dram_tensor("q_table", [N_PAD, EMBED], F32).ap()
        y_table = nc.dram_tensor("y_table", [N_PAD, EMBED], F32).ap()
        skip_table = nc.dram_tensor("skip_table", [N_PAD, EMBED], F32).ap()
        dst_rows = nc.dram_tensor("dst_rows", [CHUNKS, CHUNK // 2], F32).ap()
        new_rows = nc.dram_tensor("new_rows", [CHUNKS, CHUNK // 2], F32).ap()
        s_io = whole.enter_context(nc.semaphore("s_io"))
        K = Constants(nc, whole)
        K.turn_pe = s_turn[1]
        load_constants(nc, a, K, dst_rows, new_rows)
        window_places(nc, a, K, TILES)
        nodes_before_attention(nc, a, K, kv_table, q_table)
        with ExitStack() as one:
            acc = one.enter_context(nc.sbuf_tensor("attn_sum", [ROWS, AGG0, N_PAD], F32))
            attention_edges(nc, a, K, acc, kv_table, q_table, dst_rows, new_rows, s_turn, TILES, P, 4)
            nodes_between(nc, a, K, acc, y_table, skip_table)
        window_places(nc, a, K, 4)
        with ExitStack() as two:
            acc = two.enter_context(nc.sbuf_tensor("conv_sum", [P, AGG1, N_PAD], F32))
            convolution_edges(nc, a, K, acc, y_table, s_turn, 4, 64)
            nodes_after(nc, a, K, acc, skip_table)


class Constants:

    def __init__(self, nc, ctx):
        def sb(name, shape, dt=F32):
            return ctx.enter_context(nc.sbuf_tensor(name, shape, dt))

        self.ident = sb("ident", [P, P])
        self.iota = sb("iota", [P, P])
        self.place = sb("place", [HEADS, AGG0, ROWS])
        self.dst_rel = sb("dst_rel", [P, EDGE_TILES])
        self.part = sb("part", [P, 1])
        self.first = sb("first", [1, EDGE_TILES], I32)
        self.fold = sb("fold", [P, MUL])


class Count:

    def __init__(self, eng, sem):
        self.eng, self.sem, self.n = eng, sem, 0

    def __call__(self, ins):
        self.n += 1
        ins.then_inc(self.sem, 1)
        self.eng.wait_ge(self.sem, self.n)


def wait_then(eng, sem, value, turn):
    eng.wait_ge(sem, value)
    eng.sem_inc(turn, 1)


def load_constants(nc, a, K, dst_rows, new_rows):
    with ExitStack() as ctx:
        def sb(name, shape, dt=F32):
            return ctx.enter_context(nc.sbuf_tensor(name, shape, dt))

        lin_i = sb("lin_i", [CHUNKS, CHUNK + 1], I32)
        lin = sb("lin", [CHUNKS, CHUNK + 1])
        rel = sb("rel", [CHUNKS, CHUNK], BF16)
        new = sb("new_line", [CHUNKS, CHUNK], BF16)
        s_in = ctx.enter_context(nc.semaphore("s_in"))
        s_v = ctx.enter_context(nc.semaphore("s_prep"))
        s_out = ctx.enter_context(nc.semaphore("s_prep_out"))
        block = ctx.enter_context(nc.Block())

        @block.sync
        def _(sp):
            for dst, src in ((lin_i[:, :], a["dst_line"]), (K.ident[:, :], a["ident"]),
                             (K.iota[:, :], a["iota"].to_broadcast([P, P])), (K.place[:, :, :], a["place"]),
                             (K.first[:, :], a["first"]), (K.fold[:, :], a["fold"]), (K.part[:, :], a["part"])):
                sp.dma_start(dst, src).then_inc(s_in, 16)
            sp.wait_ge(s_v, 4)
            sp.dma_start(dst_rows, rel[:, :].bitcast(F32)).then_inc(s_out, 16)
            sp.dma_start(new_rows, new[:, :].bitcast(F32)).then_inc(s_out, 16)
            sp.wait_ge(s_out, 32)

        @block.vector
        def _(v):
            step = Count(v, s_v)
            v.wait_ge(s_in, 16 * 7)
            step(v.tensor_copy(lin[:, :], lin_i[:, :]))
            step(v.tensor_scalar(rel[:, :], lin[:, 1:CHUNK + 1], lin[:, 1:2], None, ALU.subtract))
            step(v.tensor_tensor(new[:, :], lin[:, 1:CHUNK + 1], lin[:, 0:CHUNK], ALU.not_equal))
            step(v.tensor_scalar(new[:, :], new[:, :], NEG, None, ALU.mult))


def window_places(nc, a, K, per):
    with ExitStack() as ctx:
        dst_t = ctx.enter_context(nc.sbuf_tensor(f"dst_t{per}", [P, EDGE_TILES], I32))
        first_t = ctx.enter_context(nc.sbuf_tensor(f"first_t{per}", [P, EDGE_TILES], I32))
        first_f = ctx.enter_context(nc.sbuf_tensor(f"first_f{per}", [P, EDGE_TILES], F32))
        s_in = ctx.enter_context(nc.semaphore(f"p_in{per}"))
        s_v = ctx.enter_context(nc.semaphore(f"p_step{per}"))
        block = ctx.enter_context(nc.Block())

        @block.sync
        def _(sp):
            sp.dma_start(first_t[:, :], a["first"].to_broadcast([P, EDGE_TILES])).then_inc(s_in, 16)
            sp.dma_start(dst_t[:, :], a["dst_tile"]).then_inc(s_in, 16)

        @block.vector
        def _(v):
            step = Count(v, s_v)
            v.wait_ge(s_in, 32)
            step(v.tensor_copy(first_f[:, :], first_t[:, :]))
            step(v.tensor_tensor(K.dst_rel[:, :].rearrange("p (g t) -> p g t", t=per),
                                 dst_t[:, :].rearrange("p (g t) -> p g t", t=per),
                                 first_f[:, 0:EDGE_TILES:per].unsqueeze(2).to_broadcast([P, EDGE_TILES // per, per]),
                                 ALU.subtract))


def layer_stats(v, stats, mean, rstd, tmp, step):
    cnt = EMBED
    me, mo = stats[:, :, 1], stats[:, :, 4]
    step(v.tensor_tensor(mean[:, :], me, mo, ALU.add))
    step(v.tensor_scalar(mean[:, :], mean[:, :], 0.5, None, ALU.mult))
    step(v.tensor_tensor(tmp[:, :], me, mo, ALU.subtract))
    step(v.tensor_tensor(tmp[:, :], tmp[:, :], tmp[:, :], ALU.mult))
    step(v.tensor_tensor(rstd[:, :], stats[:, :, 2], stats[:, :, 5], ALU.add))
    step(v.tensor_scalar(rstd[:, :], rstd[:, :], 1.0 / cnt, EPS, ALU.mult, ALU.add))
    step(v.scalar_tensor_tensor(out=rstd[:, :], in0=tmp[:, :], scalar=0.25, in1=rstd[:, :],
                                op0=ALU.mult, op1=ALU.add))



class NodePass:

    def __init__(self, nc, ctx, name, K, x_sb, w_sb, width):
        def sb(n, shape):
            return ctx.enter_context(nc.sbuf_tensor(f"{name}_{n}", shape, F32))

        def sem(n):
            return ctx.enter_context(nc.semaphore(f"{name}_{n}"))

        self.K, self.x_sb, self.w_sb, self.width = K, x_sb, w_sb, width
        self.h = sb("h", [P, 2, EMBED])
        self.hT = sb("hT", [P, 2, 2, P])
        self.stats = sb("stats", [P, NODE_TILES, 6])
        self.shift, self.scale, self.tmp = (sb(n, [P, NODE_TILES]) for n in ("shift", "scale", "tmp"))
        self.ps_t = [ctx.enter_context(nc.psum_tensor(f"{name}_turned{i}", [P, 2, P], F32)) for i in range(2)]
        self.ps_m = [ctx.enter_context(nc.psum_tensor(f"{name}_prod{i}", [P, 512 * -(-width // 512)], F32))
                     for i in range(2)]
        self.s_step, self.s_var, self.s_root, self.s_norm = sem("step"), sem("var"), sem("root"), sem("norm")
        self.s_stat, self.s_h, self.s_turned, self.s_copied = (
            sem(n) for n in ("s_stat", "s_h", "s_turned", "s_copied"))
        self.s_prod = [sem(f"s_prod{i}") for i in range(2)]
        self.s_taken = [sem(f"s_taken{i}") for i in range(2)]

    def statistics(self, v, step):
        with v.Fori(0, NODE_TILES) as i:
            v.bn_stats(self.stats[:, bass.ds(i, 1), :].rearrange("p a s -> p (a s)"),
                       self.x_sb[:, bass.ds(i, 1), :].rearrange("p a s -> p (a s)")).then_inc(self.s_stat, 1)
        v.wait_ge(self.s_stat, NODE_TILES)
        layer_stats(v, self.stats, self.shift, self.scale, self.tmp, step)
        v.sem_inc(self.s_var, 1)
        v.wait_ge(self.s_root, 1)
        step(v.reciprocal(self.scale[:, :], self.scale[:, :]))
        step(v.scalar_tensor_tensor(out=self.shift[:, :], in0=self.shift[:, :], scalar=-1.0,
                                    in1=self.scale[:, :], op0=ALU.mult, op1=ALU.mult))
        v.sem_inc(self.s_norm, 1)

    def scalar(self, act):
        act.wait_ge(self.s_var, 1)
        act.activation(self.scale[:, :], self.scale[:, :], ACT.Sqrt).then_inc(self.s_root, 1)
        act.wait_ge(self.s_norm, 1)

        def relu(j, s):
            act.activation(self.h[:, s, :], self.x_sb[:, bass.ds(j, 1), :].rearrange("p a f -> p (a f)"),
                           ACT.Relu, bias=self.shift[:, bass.ds(j, 1)],
                           scale=self.scale[:, bass.ds(j, 1)]).then_inc(self.s_h, 1)

        def copy(j, s, rounds):
            act.wait_ge(self.s_turned, j + 1)
            act.wait_ge(self.s_prod[s], rounds)
            act.activation(self.hT[:, s, :, :], self.ps_t[s][:, :, :], ACT.Copy).then_inc(self.s_copied, 1)

        relu(0, 0)
        with act.Fori(0, NODE_TILES // 2 - 1) as i:
            for s in range(2):
                act.wait_ge(self.s_turned, 2 * i + s)
                relu(2 * i + s + 1, 1 - s)
                copy(2 * i + s, s, i)
        last = NODE_TILES - 2
        act.wait_ge(self.s_turned, last)
        relu(last + 1, 1)
        copy(last, 0, last // 2)
        copy(last + 1, 1, last // 2)

    def tensor(self, pe):
        def turn(j, s):
            pe.wait_ge(self.s_h, j + 1)
            for c in range(2):
                mm = pe.transpose(self.ps_t[s][:, c, :], self.h[:, s, c * P:(c + 1) * P], self.K.ident[:, :])
            mm.then_inc(self.s_turned, 1)

        def project(j, s, rounds):
            pe.wait_ge(self.s_copied, j + 1)
            pe.wait_ge(self.s_taken[s], rounds)
            for n in range(0, self.width, 512):
                m = min(self.width, n + 512)
                for c in range(2):
                    mm = pe.matmul(self.ps_m[s][:, n:m], self.hT[:, s, c, :], self.w_sb[:, c, n:m],
                                   start=c == 0, stop=c == 1)
            mm.then_inc(self.s_prod[s], 1)

        turn(0, 0)
        with pe.Fori(0, NODE_TILES // 2 - 1) as i:
            for s in range(2):
                turn(2 * i + s + 1, 1 - s)
                project(2 * i + s, s, i)
        last = NODE_TILES - 2
        turn(last + 1, 1)
        project(last, 0, last // 2)
        project(last + 1, 1, last // 2)


def nodes_before_attention(nc, a, K, kv_table, q_table):
    WID = 3 * EMBED
    with ExitStack() as ctx:
        def sb(name, shape, dt=F32):
            return ctx.enter_context(nc.sbuf_tensor(name, shape, dt))

        def sem(name):
            return ctx.enter_context(nc.semaphore(name))

        x_sb = sb("x_sb", [P, NODE_TILES, EMBED])
        w_sb = sb("w_sb", [P, 2, WID])
        b_sb = sb("b_sb", [P, WID])
        o_sb = sb("o_sb", [P, 2, WID])
        N = NodePass(nc, ctx, "pre", K, x_sb, w_sb, WID)
        s_x, s_w, s_scaled = sem("s_x"), sem("s_w"), sem("s_scaled")
        s_stored = [sem(f"s_stored{i}") for i in range(2)]
        block = ctx.enter_context(nc.Block())
        x_d = a["x"].rearrange("(i p) f -> p i f", p=P)
        h = NODE_TILES // 2

        @block.sync
        def _(sp):
            sp.dma_start(x_sb[:, 0:h, :], x_d[:, 0:h, :]).then_inc(s_x, 16)
            sp.dma_start(x_sb[:, h:NODE_TILES, :], x_d[:, h:NODE_TILES, :]).then_inc(s_x, 16)
            sp.dma_start(w_sb[:, :, :], a["wqkv"]).then_inc(s_w, 16)
            sp.dma_start(b_sb[:, :], a["bqkv"].to_broadcast([P, WID])).then_inc(s_w, 16)
            with sp.Fori(0, h) as i:
                for s in range(2):
                    sp.wait_ge(N.s_taken[s], i + 1)
                    row = bass.ds((2 * i + s) * P, P)
                    sp.dma_start(kv_table[row, :], o_sb[:, s, 0:2 * EMBED]).then_inc(s_stored[s], 16)
                    sp.dma_start(q_table[row, :], o_sb[:, s, 2 * EMBED:WID]).then_inc(s_stored[s], 16)
            for s in range(2):
                sp.wait_ge(s_stored[s], 32 * h)

        @block.vector
        def _(v):
            step = Count(v, N.s_step)
            v.wait_ge(s_w, 32)
            step(v.tensor_scalar(w_sb[:, :, 2 * EMBED:WID], w_sb[:, :, 2 * EMBED:WID], HDIM ** -0.5, None, ALU.mult))
            step(v.tensor_scalar(b_sb[:, 2 * EMBED:WID], b_sb[:, 2 * EMBED:WID], HDIM ** -0.5, None, ALU.mult))
            v.sem_inc(s_scaled, 1)
            v.wait_ge(s_x, 32)
            N.statistics(v, step)
            with v.Fori(0, h) as i:
                for s in range(2):
                    v.wait_ge(N.s_prod[s], i + 1)
                    v.wait_ge(s_stored[s], 32 * i)
                    v.tensor_tensor(o_sb[:, s, :], N.ps_m[s][:, 0:WID], b_sb[:, :],
                                    ALU.add).then_inc(N.s_taken[s], 1)

        @block.scalar
        def _(act):
            N.scalar(act)

        @block.tensor
        def _(pe):
            pe.wait_ge(s_scaled, 1)
            N.tensor(pe)


def attention_edges(nc, a, K, acc, kv_table, q_table, dst_rows, new_rows, s_turn, per, W, R):
    GR = TILES // per
    ABREAST = P // W
    fold = K.fold if W == MUL else K.ident
    turn_pool, turn_pe = s_turn
    with ExitStack() as ctx:
        def sb(name, shape, dt=F32):
            return ctx.enter_context(nc.sbuf_tensor(name, shape, dt))

        def sem(name):
            return ctx.enter_context(nc.semaphore(name))

        def psum(name, shape):
            return ctx.enter_context(nc.psum_tensor(name, shape, F32))

        kv = sb("kv", [P, R, TILES, 2 * EMBED])
        idx = sb("idx", [P, R, TILES], I32)
        rows = sb("rows", [P, 2, CHUNK], BF16)
        new = sb("new", [HEADS, 2, CHUNK], BF16)
        qw = sb("qw", [P, 2, EMBED])
        sel = sb("sel", [P, 2, TILES, W])
        selT = sb("selT", [P, CHUNK])
        prod = sb("prod", [P, 2, HALF, EMBED])
        score = sb("score", [P, 2, TILES * HEADS])
        top = sb("top", [HEADS, 2, CHUNK])
        diff = sb("diff", [P, TILES * HEADS])
        msg = sb("msg", [P, 2, TILES, MSG])
        fall = sb("fall", [HEADS, 1])
        fade = sb("fade", [HEADS, 1])
        ps_q = [psum(f"ps_q{h}", [P, HALF, EMBED]) for h in range(2)]
        ps_s = psum("ps_s", [P, CHUNK])
        part = sb("part_sums", [P, 2, MSG])
        ps_p = psum("ps_p", [P, 512])
        ps_a = psum("ps_a", [P, 512])
        turned = ps_a[0:ROWS, 0:AGG0 * W].rearrange("p (k w) -> p k w", w=W)
        ps_top = ps_s[:, 0:TILES * HEADS]
        ps_fade = ps_a[0:ROWS, 448:448 + AGG0]

        s_idx = [sem(f"s_idx{r}") for r in range(R)]
        s_kv = [sem(f"s_kv{r}") for r in range(R)]
        s_kv_used = [sem(f"s_kv_used{r}") for r in range(R)]
        s_rows = [sem(f"s_rows{u}") for u in range(2)]
        s_rows_used = [sem(f"s_rows_used{u}") for u in range(2)]
        s_new = [sem(f"s_new{u}") for u in range(2)]
        s_new_used = [sem(f"s_new_used{u}") for u in range(2)]
        (s_zero, s_selT, s_sel, s_q, s_mul, s_score, s_scoreT, s_run, s_top, s_topT, s_diff, s_fall, s_fade,
         s_fadeR, s_exp, s_faded, s_msg, s_part, s_kept, s_agg, s_sum, s_far, s_farT) = (sem("s_" + n) for n in (
             "zero", "selT", "sel", "q", "mul", "score", "scoreT", "run", "top", "topT", "diff", "fall", "fade",
             "fadeR", "exp", "faded", "msg", "part", "kept", "agg", "sum", "far", "farT"))
        block = ctx.enter_context(nc.Block())
        U = UNROLL
        src_d = a["src_line"]

        @block.sync
        def _(sp):
            with sp.Fori(0, CHUNKS // U) as i:
                for m in range(U):
                    c, r, u, k = U * i + m, m % R, m % 2, i * (U // 2) + m // 2
                    n0 = sp.value_load(K.first[0:1, bass.ds(c * TILES, 1)], min_val=0, max_val=N_NODES)
                    sp.wait_ge(s_kv[r], (i * (U // R) + m // R) * 16 * TILES)
                    sp.dma_start(idx[:, r, :], src_d[bass.ds(c, 1), :, :].rearrange("a p t -> p (a t)")
                                 ).then_inc(s_idx[r], 16)
                    sp.wait_ge(s_rows_used[u], k)
                    row = bass.ds(c, 1)
                    sp.dma_start(rows[:, u, :].bitcast(F32), dst_rows[row, :].to_broadcast([P, CHUNK // 2])).then_inc(s_rows[u], 16)
                    sp.dma_start(qw[:, u, :], q_table[bass.ds(n0, P), :]).then_inc(s_rows[u], 16)
                    sp.wait_ge(s_new_used[u], k)
                    sp.dma_start(new[:, u, :].bitcast(F32), new_rows[row, :].to_broadcast([HEADS, CHUNK // 2])).then_inc(s_new[u], 16)

        @block.gpsimd
        def _(gp):
            with gp.Fori(0, CHUNKS // U) as i:
                for m in range(U):
                    r, k = m % R, i * (U // R) + m // R
                    wait_then(gp, s_idx[r], 16 * (k + 1), turn_pool)
                    wait_then(gp, s_kv_used[r], k, turn_pool)
                    for t in range(TILES):
                        gp.indirect_dma_start(kv[:, r, t, :], None, kv_table,
                                              bass.IndirectOffsetOnAxis(ap=idx[:, r, t:t + 1].bitcast(U32), axis=0)
                                              ).then_inc(s_kv[r], 16)

        @block.vector
        def _(v):
            v.memset(acc[:, :, :], 0.0).then_inc(s_zero, 1)
            v.memset(top[:, 1, CHUNK - 1:CHUNK], NEG).then_inc(s_zero, 1)
            v.wait_ge(s_zero, 2)

            def multiply(c, r, k):
                v.wait_ge(s_kv[r], 16 * TILES * (k + 1))
                for h in range(2):
                    v.wait_ge(s_q, 2 * c + h + 1)
                    v.tensor_tensor(prod[:, h, :, :], kv[:, r, h * HALF:(h + 1) * HALF, 0:EMBED],
                                    ps_q[h][:, :, :], ALU.mult).then_inc(s_mul, 1)

            def add_up(c, h, u):
                v.wait_ge(s_mul, 2 * c + h + 1)
                v.tensor_reduce(score[:, u, h * HALF * HEADS:(h + 1) * HALF * HEADS],
                                prod[:, h, :, :].rearrange("p t (h d) -> p (t h) d", d=HDIM),
                                AX_X, ALU.add).then_inc(s_score, 1)

            def weigh(c, u):
                v.wait_ge(s_topT, c + 1)
                v.wait_ge(s_exp, c)
                v.tensor_tensor(diff[:, :], score[:, u, :], ps_top, ALU.subtract).then_inc(s_diff, 1)

            def run(c, u, k):
                v.wait_ge(s_scoreT, c + 1)
                v.wait_ge(s_new[u], 16 * (k + 1))
                v.wait_ge(s_top, c)
                v.tensor_tensor_scan(top[:, u, :], new[:, u, :], ps_s[0:HEADS, :], top[:, 1 - u, CHUNK - 1:CHUNK],
                                     ALU.add, ALU.max).then_inc(s_run, 1)

            def spread(c, u):
                v.wait_ge(s_run, c + 1)
                v.tensor_tensor_scan(top[:, u, CHUNK - 2::-1], new[:, u, CHUNK - 1:0:-1], top[:, u, CHUNK - 2::-1],
                                     top[:, u, CHUNK - 1:CHUNK], ALU.add, ALU.max).then_inc(s_top, 1)

            def rise(c, u):
                v.wait_ge(s_top, c + 1)
                v.wait_ge(s_fade, c)
                v.tensor_scalar(fall[:, :], top[:, 1 - u, CHUNK - 1:CHUNK], top[:, u, 0:1], 0.0,
                                ALU.subtract, ALU.min).then_inc(s_fall, 1)
                v.sem_inc(s_new_used[u], 1)

            def messages(c, h, r, u):
                v.wait_ge(s_exp, c + 1)
                t = slice(h * HALF, (h + 1) * HALF)
                v.tensor_tensor(msg[:, u, t, HEADS:MSG].rearrange("p t (h d) -> p t h d", d=HDIM),
                                kv[:, r, t, EMBED:2 * EMBED].rearrange("p t (h d) -> p t h d", d=HDIM),
                                msg[:, u, t, 0:HEADS].unsqueeze(3).to_broadcast([P, HALF, HEADS, HDIM]),
                                ALU.mult).then_inc(s_msg, 1)

            def first(c, g):
                return v.value_load(K.first[0:1, bass.ds(c * TILES + g * per, 1)], min_val=0, max_val=N_NODES)

            def fade_sums(c):
                n0 = first(c, 0)
                v.wait_ge(s_fadeR, c + 1)
                v.wait_ge(s_sum, GR * c)
                v.tensor_tensor(acc[:, :, bass.ds(n0, 1)], acc[:, :, bass.ds(n0, 1)], ps_fade.unsqueeze(2),
                                ALU.mult).then_inc(s_faded, 1)
                v.wait_ge(s_faded, c + 1)

            def sums(c, g):
                n0 = first(c, g)
                v.wait_ge(s_agg, GR * c + g + 1)
                v.wait_ge(s_sum, GR * c + g)
                v.tensor_tensor(acc[:, :, bass.ds(n0, W)], acc[:, :, bass.ds(n0, W)], turned,
                                ALU.add).then_inc(s_sum, 1)

            def chunk(c, j, i):
                u, now, past, older = j % 2, exists(c), exists(c - 1), exists(c - 2)
                if past:
                    rise(c - 1, 1 - u)
                    weigh(c - 1, 1 - u)
                if older:
                    v.wait_ge(s_msg, 2 * (c - 1))
                    v.sem_inc(s_kv_used[(j - 2) % R], 1)
                if now:
                    multiply(c, j % R, i * (U // R) + j // R)
                if now:
                    add_up(c, 0, u)
                    add_up(c, 1, u)
                if older:
                    for g in range(GR - 1):
                        sums(c - 2, g)
                if past:
                    messages(c - 1, 0, (j - 1) % R, 1 - u)
                if now:
                    run(c, u, i * (U // 2) + j // 2)
                if older:
                    sums(c - 2, GR - 1)
                if now:
                    spread(c, u)
                if past:
                    fade_sums(c - 1)
                    messages(c - 1, 1, (j - 1) % R, 1 - u)

            walk(v, chunk)

        @block.scalar
        def _(act):
            def select_turned(c, u, k):
                act.wait_ge(s_rows[u], 32 * (k + 1))
                act.wait_ge(s_q, 2 * c)
                act.activation(selT[:, :], rows[:, u, :], ACT.Square, scale=-1.0, bias=K.part[:, 0:1]).then_inc(s_farT, 1)
                act.wait_ge(s_farT, c + 1)
                act.activation(selT[:, :], selT[:, :], ACT.Relu, scale=-1.0, bias=1.0).then_inc(s_selT, 1)

            def select(c, u):
                if exists(c - 2):
                    act.wait_ge(s_part, GR * (c - 1))
                for t in range(TILES):
                    ins = act.activation(sel[:, u, t, :], K.iota[:, 0:W], ACT.Square, scale=-1.0,
                                         bias=K.dst_rel[:, bass.ds(c * TILES + t, 1)])
                ins.then_inc(s_far, 1)
                act.wait_ge(s_far, c + 1)
                act.activation(sel[:, u, :, :], sel[:, u, :, :], ACT.Relu, scale=-1.0, bias=1.0).then_inc(s_sel, 1)

            def chunk(c, j, i):
                if j == 0 and c == 0:
                    select_turned(0, 0, 0)
                if exists(c - 1):
                    act.wait_ge(s_fall, c)
                    act.wait_ge(s_fadeR, c - 1)
                    act.activation(fade[:, :], fall[:, :], ACT.Exp).then_inc(s_fade, 1)
                    act.wait_ge(s_diff, c)
                    if exists(c - 3):
                        act.wait_ge(s_part, GR * (c - 2))
                    act.activation(msg[:, (j - 1) % 2, :, 0:HEADS], diff[:, :].rearrange("p (t h) -> p t h", h=HEADS),
                                   ACT.Exp).then_inc(s_exp, 1)
                if exists(c + 1):
                    select_turned(c + 1, (j + 1) % 2, i * (U // 2) + (j + 1) // 2)
                if exists(c - 2):
                    for g in range(GR):
                        act.wait_ge(s_part, GR * (c - 2) + g + 1)
                        if exists(c - 3) or g > 0:
                            act.wait_ge(s_agg, GR * (c - 2) + g)
                        act.activation(part[:, 0, :], ps_p[:, 0:MSG], ACT.Copy).then_inc(s_kept, 1)

                if exists(c - 1):
                    select(c - 1, (j - 1) % 2)

            walk(act, chunk)

        @block.tensor
        def _(pe):
            def queries(c, h, u, k):
                pe.wait_ge(s_rows[u], 32 * (k + 1))
                pe.wait_ge(s_selT, c + 1)
                if not isinstance(c, int) or c > 0:
                    pe.wait_ge(s_mul, 2 * c - 1 + h)
                for t in range(HALF):
                    mm = pe.matmul(ps_q[h][:, t, :], selT[:, (h * HALF + t) * P:(h * HALF + t + 1) * P],
                                   qw[:, u, :], start=True, stop=True)
                mm.then_inc(s_q, 1)

            def sums(c, g, u):
                pe.wait_ge(s_msg, 2 * c + 2)
                pe.wait_ge(s_sel, c + 1)
                pe.wait_ge(s_kept, GR * c + g)
                for t in range(per):
                    at = t % ABREAST * W
                    mm = pe.matmul(ps_p[at:at + W, 0:MSG], sel[:, u, g * per + t, :], msg[:, u, g * per + t, :],
                                   start=t < ABREAST, stop=t >= per - ABREAST, skip_group_check=True)
                mm.then_inc(s_part, 1)

            def turn_sums(c, g):
                pe.wait_ge(s_kept, GR * c + g + 1)
                pe.wait_ge(s_sum, GR * c + g)
                if g == 0:
                    pe.wait_ge(s_faded, c + 1)
                for m in range(AGG0):
                    mm = pe.matmul(turned[:, m, :], part[:, 0, m * ROWS:(m + 1) * ROWS], fold[:, :],
                                   start=True, stop=True)
                mm.then_inc(s_agg, 1)

            def turn_scores(c, u):
                pe.wait_ge(s_score, 2 * c + 2)
                pe.wait_ge(s_diff, c)
                for t in range(TILES):
                    mm = pe.transpose(ps_s[0:HEADS, t * P:(t + 1) * P],
                                      score[:, u, t * HEADS:(t + 1) * HEADS], K.ident[:, :])
                mm.then_inc(s_scoreT, 1)

            def turn_top(c, u):
                wait_then(pe, s_top, c + 1, turn_pe)
                for t in range(TILES):
                    mm = pe.transpose(ps_top[:, t * HEADS:(t + 1) * HEADS], top[:, u, t * P:(t + 1) * P],
                                      K.ident[0:HEADS, 0:HEADS])
                mm.then_inc(s_topT, 1)

            def spread_fade(c):
                wait_then(pe, s_faded, c, turn_pe)
                wait_then(pe, s_fade, c + 1, turn_pe)
                for m in range(AGG0):
                    mm = pe.matmul(ps_fade[:, m:m + 1], K.place[:, m, :], fade[:, :], start=True, stop=True)
                mm.then_inc(s_fadeR, 1)

            def chunk(c, j, i):
                if j == 0 and c == 0:
                    queries(0, 0, 0, 0)
                if exists(c - 1):
                    turn_top(c - 1, (j - 1) % 2)
                if exists(c):
                    queries(c, 1, j % 2, i * (U // 2) + j // 2)
                if exists(c - 2):
                    sums(c - 2, 0, j % 2)
                if exists(c):
                    wait_then(pe, s_q, 2 * c + 2, turn_pe)
                    pe.sem_inc(s_rows_used[j % 2], 1)
                if exists(c - 1):
                    spread_fade(c - 1)
                if exists(c - 2):
                    for g in range(1, GR):
                        turn_sums(c - 2, g - 1)
                        sums(c - 2, g, j % 2)
                if exists(c):
                    turn_scores(c, j % 2)
                if exists(c - 2):
                    turn_sums(c - 2, GR - 1)
                if exists(c + 1):
                    queries(c + 1, 0, (j + 1) % 2, i * (U // 2) + (j + 1) // 2)

            walk(pe, chunk)


def exists(c):
    return not isinstance(c, int) or 0 <= c < CHUNKS


def walk(eng, chunk):
    for c in range(2):
        chunk(c, c, 0)
    with eng.Fori(0, CHUNKS // UNROLL - 1) as i:
        for j in range(2, UNROLL + 2):
            chunk(UNROLL * i + j, j, i)
    for c in range(CHUNKS - 2, CHUNKS + 2):
        chunk(c, c % UNROLL, c // UNROLL)


def nodes_between(nc, a, K, acc, y_table, skip_table):
    WID = 2 * EMBED
    with ExitStack() as ctx:
        def sb(name, shape, dt=F32):
            return ctx.enter_context(nc.sbuf_tensor(name, shape, dt))

        def sem(name):
            return ctx.enter_context(nc.semaphore(name))

        x_sb = sb("x1_sb", [P, NODE_TILES, EMBED])
        w_sb = sb("w1_sb", [P, 2, WID])
        wo = sb("wo", [ROWS, AGG0, EMBED])
        bo = sb("bo", [P, EMBED])
        nv = sb("nv", [P, NODE_TILES])
        mean_v = sb("mean_v", [ROWS, 2, AGG0, P])
        y_sb = sb("y_sb", [P, 2, EMBED])
        N = NodePass(nc, ctx, "mid", K, x_sb, w_sb, WID)
        ps_r = N.ps_m
        ps_o = N.ps_t
        s_x, s_w, s_y, s_skip, s_scaled, s_recip = (
            sem(n) for n in ("m_x", "m_w", "m_y", "m_skip", "m_scaled", "m_recip"))
        s_spread, s_mean, s_out, s_added, s_res, s_bias = (
            sem(n) for n in ("m_spread", "m_mean", "m_out", "m_added", "m_res", "m_bias"))
        s_stored = [sem(f"m_stored{i}") for i in range(2)]
        block = ctx.enter_context(nc.Block())
        h = NODE_TILES // 2

        @block.sync
        def _(sp):
            sp.dma_start(x_sb[:, :, :], a["x"].rearrange("(i p) f -> p i f", p=P)).then_inc(s_x, 16)
            for dst, src in ((w_sb[:, :, :], a["wys"]), (wo[:, :, :], a["wo"]), (nv[:, :], a["nv"]),
                             (bo[:, :], a["bo"].to_broadcast([P, EMBED]))):
                sp.dma_start(dst, src).then_inc(s_w, 16)
            with sp.Fori(0, h) as i:
                for s in range(2):
                    sp.wait_ge(N.s_taken[s], i + 1)
                    sp.dma_start(y_table[bass.ds((2 * i + s) * P, P), :], y_sb[:, s, :]).then_inc(s_stored[s], 16)
                    sp.dma_start(skip_table[bass.ds((2 * i + s) * P, P), :],
                                 x_sb[:, bass.ds(2 * i + s, 1), :].rearrange("p a f -> p (a f)")
                                 ).then_inc(s_stored[s], 16)
            for s in range(2):
                sp.wait_ge(s_stored[s], 32 * h)

        @block.vector
        def _(v):
            step = Count(v, N.s_step)
            step(v.tensor_scalar(acc[0:HEADS, 0, :], acc[0:HEADS, 0, :], 1e-15, None, ALU.max))
            v.reciprocal(acc[0:HEADS, 0, :], acc[0:HEADS, 0, :]).then_inc(s_recip, 1)
            v.wait_ge(s_recip, 1)
            v.wait_ge(s_w, 64)
            step(v.tensor_scalar(w_sb[:, :, 0:EMBED], w_sb[:, :, 0:EMBED], MUL ** -0.5, None, ALU.mult))
            step(v.tensor_scalar(w_sb[:, :, EMBED:WID], w_sb[:, :, EMBED:WID],
                                 math.sin(math.pi / 8.0) * MUL ** -0.5, None, ALU.mult))
            v.sem_inc(s_scaled, 1)
            v.wait_ge(s_x, 16)

            def normalise(j, s):
                v.wait_ge(s_spread, j + 1)
                v.tensor_tensor(mean_v[:, s, :, :], acc[:, :, bass.ds(j * P, P)],
                                ps_r[s][0:ROWS, 0:AGG0 * P].rearrange("p (k n) -> p k n", n=P),
                                ALU.mult).then_inc(s_mean, 1)

            def add(j, s):
                row = x_sb[:, bass.ds(j, 1), :].rearrange("p a f -> p (a f)")
                v.wait_ge(s_out, j + 1)
                v.tensor_tensor(row, row, ps_o[s][:, :, :].rearrange("p a b -> p (a b)"), ALU.add).then_inc(s_added, 1)

            normalise(0, 0)
            with v.Fori(0, h - 1) as i:
                for s in range(2):
                    normalise(2 * i + s + 1, 1 - s)
                    add(2 * i + s, s)
            normalise(NODE_TILES - 1, 1)
            add(NODE_TILES - 2, 0)
            add(NODE_TILES - 1, 1)
            v.wait_ge(s_added, NODE_TILES)
            step(v.tensor_tensor(x_sb[:, :, :], x_sb[:, :, :],
                                 bo[:, :].unsqueeze(1).to_broadcast([P, NODE_TILES, EMBED]), ALU.add))
            N.statistics(v, step)
            with v.Fori(0, h) as i:
                for s in range(2):
                    j = 2 * i + s
                    row = x_sb[:, bass.ds(j, 1), :].rearrange("p a f -> p (a f)")
                    v.wait_ge(N.s_prod[s], i + 1)
                    v.wait_ge(s_stored[s], 32 * i)
                    v.tensor_scalar(y_sb[:, s, :], N.ps_m[s][:, 0:EMBED], nv[:, bass.ds(j, 1)], None,
                                    ALU.mult).then_inc(s_y, 1)
                    v.wait_ge(s_y, j + 1)
                    v.scalar_tensor_tensor(out=row, in0=N.ps_m[s][:, EMBED:WID], scalar=nv[:, bass.ds(j, 1)],
                                           in1=row, op0=ALU.mult, op1=ALU.add).then_inc(N.s_taken[s], 1)

        @block.scalar
        def _(act):
            N.scalar(act)

        @block.tensor
        def _(pe):
            pe.wait_ge(s_w, 64)
            pe.wait_ge(s_recip, 1)
            pe.wait_ge(s_scaled, 1)

            def spread(j, s):
                pe.sem_inc(K.turn_pe, 1)
                for k in range(AGG0):
                    mm = pe.matmul(ps_r[s][0:ROWS, k * P:(k + 1) * P], K.place[:, k, :],
                                   acc[0:HEADS, 0, bass.ds(j * P, P)], start=True, stop=True)
                mm.then_inc(s_spread, 1)

            def out(j, s):
                pe.wait_ge(s_mean, j + 1)
                for k in range(AGG0):
                    mm = pe.matmul(ps_o[s][:, :, :].rearrange("p a b -> p (a b)"), mean_v[:, s, k, :], wo[:, k, :],
                                   start=k == 0, stop=k == AGG0 - 1)
                mm.then_inc(s_out, 1)

            spread(0, 0)
            with pe.Fori(0, h - 1) as i:
                for s in range(2):
                    pe.wait_ge(s_added, 2 * i)
                    spread(2 * i + s + 1, 1 - s)
                    out(2 * i + s, s)
            pe.wait_ge(s_added, NODE_TILES - 2)
            spread(NODE_TILES - 1, 1)
            out(NODE_TILES - 2, 0)
            out(NODE_TILES - 1, 1)
            N.tensor(pe)


def convolution_edges(nc, a, K, acc, y_table, s_turn, per, W):
    GR = EDGE_TILES // per
    U = 4
    with ExitStack() as ctx:
        def sb(name, shape, dt=F32):
            return ctx.enter_context(nc.sbuf_tensor(name, shape, dt))

        def sem(name):
            return ctx.enter_context(nc.semaphore(name))

        def psum(name, shape):
            return ctx.enter_context(nc.psum_tensor(name, shape, F32))

        y = sb("y", [P, U, per, EMBED])
        idx = sb("idx1", [P, 2, TILES], I32)
        es = sb("es", [2 * SCALARS, U, 2 * P])
        ea = sb("ea", [P, EDGE_TILES, 4])
        fc1 = sb("fc1", [2 * SCALARS, P])
        fc2 = sb("fc2", [P, 2, EMBED])
        hid = sb("hid", [P, 2, 2 * P])
        w_ad = sb("w_ad", [P, 2, per, P])
        msg = sb("msg1", [P, 2, per, EMBED + 5 * MUL])
        sel = sb("sel1", [P, 2, per, W])
        sel_ax = sb("sel_ax", [P, 2, per, 3, W])
        ps_h = [psum(f"ps_h{u}", [P, 512]) for u in range(2)]
        ps_ad = [psum(f"ps_ad{u}", [P, per, P]) for u in range(2)]
        ps_cb = [psum(f"ps_cb{u}", [P, per, P]) for u in range(2)]
        ps_a = [psum(f"ps_c{u}", [P, 512]) for u in range(2)]
        s_idx = [sem(f"c_idx{r}") for r in range(2)]
        s_y = [sem(f"c_y{r}") for r in range(U)]
        s_es = [sem(f"c_es{r}") for r in range(U)]
        (s_in, s_zero, s_hid, s_silu, s_w, s_ad, s_sel, s_ax, s_msg, s_agg, s_prep) = (
            sem("c_" + n) for n in ("in", "zero", "hid", "silu", "w", "ad", "sel", "ax", "msg", "agg", "prep"))
        s_sum = [sem(f"c_sum{u}") for u in range(2)]
        block = ctx.enter_context(nc.Block())
        turn_pool, turn_pe = s_turn

        @block.sync
        def _(sp):
            for dst, src in ((ea[:, :, :], a["ea"]), (fc1[:, :], a["fc1"]), (fc2[:, :, :], a["fc2"])):
                sp.dma_start(dst, src).then_inc(s_in, 16)
            def load(i):
                for m in range(U):
                    r = m // 2
                    if m % 2 == 0:
                        for k in range(2):
                            sp.wait_ge(s_y[m + k], i * 16 * per)
                        sp.dma_start(idx[:, r, :],
                                     a["src_line"][bass.ds(2 * i + r, 1), :, :].rearrange("a p t -> p (a t)")
                                     ).then_inc(s_idx[r], 16)
                    if not isinstance(i, int):
                        sp.wait_ge(s_hid, U * i + m - U + 1)
                    sp.dma_start(es[:, m, :], a["es"][bass.ds(U * i + m, 1), :, :].rearrange("a k n -> k (a n)")
                                 ).then_inc(s_es[m], 16)

            load(0)
            with sp.Fori(1, GR // U) as i:
                load(i)

        @block.gpsimd
        def _(gp):
            def gather(i):
                for m in range(U):
                    if m % 2 == 0:
                        wait_then(gp, s_idx[m // 2], 16 * (i + 1), turn_pool)
                    if not isinstance(i, int):
                        wait_then(gp, s_msg, U * i + m - U + 1, turn_pool)
                    for t in range(per):
                        q = (m % 2) * per + t
                        gp.indirect_dma_start(y[:, m, t, :], None, y_table,
                                              bass.IndirectOffsetOnAxis(ap=idx[:, m // 2, q:q + 1].bitcast(U32), axis=0)
                                              ).then_inc(s_y[m], 16)

            gather(0)
            with gp.Fori(1, GR // U) as i:
                gather(i)

        @block.vector
        def _(v):
            step = Count(v, s_prep)
            v.memset(acc[:, :, :], 0.0).then_inc(s_zero, 1)
            v.wait_ge(s_in, 48)
            step(v.tensor_scalar(fc2[:, :, :], fc2[:, :, :], 1.679 * MUL ** -0.5, None, ALU.mult))
            v.wait_ge(s_zero, 1)

            def messages(g, r, i):
                u = r % 2
                v.tensor_tensor(sel[:, u, :, :], K.iota[:, 0:W].unsqueeze(1).to_broadcast([P, per, W]),
                                K.dst_rel[:, bass.ds(g * per, per)].unsqueeze(2).to_broadcast([P, per, W]),
                                ALU.is_equal).then_inc(s_sel, 1)
                v.wait_ge(s_sel, g + 1)
                v.tensor_tensor(sel_ax[:, u, :, :, :],
                                sel[:, u, :, :].unsqueeze(2).to_broadcast([P, per, 3, W]),
                                ea[:, bass.ds(g * per, per), 1:4].unsqueeze(3).to_broadcast([P, per, 3, W]),
                                ALU.mult).then_inc(s_ax, 1)
                v.wait_ge(s_y[r], 16 * per * (i + 1))
                v.wait_ge(s_w, g + 1)
                y0 = y[:, r, :, 0:MUL]
                y1 = y[:, r, :, MUL:EMBED].rearrange("p t (c f) -> p t c f", c=3)
                v.tensor_tensor(msg[:, u, :, EMBED + MUL:].rearrange("p t (c f) -> p t c f", f=MUL)[:, :, 0:3:2, :],
                                ps_cb[u][:, :, 0:MUL].unsqueeze(2).to_broadcast([P, per, 2, MUL]),
                                y0.unsqueeze(2).to_broadcast([P, per, 2, MUL]), ALU.mult)
                v.tensor_tensor(msg[:, u, :, EMBED:].rearrange("p t (c f) -> p t c f", f=MUL)[:, :, 0:5:2, :],
                                ps_cb[u][:, :, MUL:P].unsqueeze(2).to_broadcast([P, per, 3, MUL]), y1, ALU.mult)
                v.wait_ge(s_ad, g + 1)
                v.tensor_tensor(msg[:, u, :, 0:MUL], w_ad[:, u, :, 0:MUL], y0, ALU.mult)
                v.tensor_tensor(msg[:, u, :, MUL:EMBED].rearrange("p t (c f) -> p t c f", c=3),
                                w_ad[:, u, :, MUL:P].unsqueeze(2).to_broadcast([P, per, 3, MUL]), y1,
                                ALU.mult).then_inc(s_msg, 1)

            def sums(g, j, i):
                u = j % 2
                n0 = v.value_load(K.first[0:1, bass.ds(g * per, 1)], min_val=0, max_val=N_NODES)
                v.wait_ge(s_agg, g + 1)
                v.wait_ge(s_sum[1 - u], 2 * i + (j + 1) // 2)
                v.tensor_tensor(acc[:, :, bass.ds(n0, W)], acc[:, :, bass.ds(n0, W)],
                                ps_a[u][:, 0:AGG1 * W].rearrange("p (k w) -> p k w", w=W),
                                ALU.add).then_inc(s_sum[u], 1)

            def group(g, j, i):
                if g is not None:
                    messages(g, j % U, i + j // U)
                if not isinstance(g, int) or g > 0:
                    sums(g - 1 if g is not None else GR - 1, j - 1, i)

            walk_groups(v, group, GR)

        @block.scalar
        def _(act):
            def silu(g, u):
                act.wait_ge(s_hid, g + 1)
                act.activation(hid[:, u, :], ps_h[u][:, 0:2 * P], ACT.Silu, scale=SCALARS ** -0.5).then_inc(s_silu, 1)

            def group(g, j, i):
                if g is None:
                    return
                if not isinstance(g, int) or g < GR - 1:
                    silu(g + 1, (j + 1) % 2)
                act.wait_ge(s_w, g + 1)
                u = j % 2
                for t in range(per):
                    ins = act.activation(w_ad[:, u, t, :], ps_ad[u][:, t, :], ACT.Copy,
                                         scale=ea[:, bass.ds(g * per + t, 1), 0:1].rearrange("p a b -> p (a b)"))
                ins.then_inc(s_ad, 1)

            act.wait_ge(s_in, 48)
            silu(0, 0)
            walk_groups(act, group, GR)

        @block.tensor
        def _(pe):
            def hidden(g, r, i):
                wait_then(pe, s_es[r], 16 * (i + 1), turn_pe)
                pe.matmul(ps_h[r % 2][:, 0:2 * P], fc1[:, :], es[:, r, :], start=True, stop=True).then_inc(s_hid, 1)

            def group(g, j, i):
                u = j % 2
                if g is not None:
                    if not isinstance(g, int) or g < GR - 1:
                        hidden(g + 1, (j + 1) % U, i + (j + 1) // U)
                    pe.wait_ge(s_silu, g + 1)
                    if not isinstance(g, int) or g > 1:
                        pe.wait_ge(s_msg, g - 1)
                    for t in range(per):
                        for q, out in enumerate((ps_ad[u], ps_cb[u])):
                            mm = pe.matmul(out[:, t, :], hid[:, u, (t % 2) * P:(t % 2 + 1) * P],
                                           fc2[:, t // 2, q * P:(q + 1) * P], start=True, stop=True)
                    mm.then_inc(s_w, 1)
                if not isinstance(g, int) or g > 0:
                    b, bu = (g - 1) if g is not None else GR - 1, (j - 1) % 2
                    pe.wait_ge(s_msg, b + 1)
                    pe.wait_ge(s_sum[bu], 2 * i + (j - 1) // 2)
                    out = ps_a[bu][:, 0:AGG1 * W].rearrange("p (k w) -> p k w", w=W)
                    for t in range(per):
                        for m in range(AGG1):
                            at = BLOCK_AT[m]
                            mm = pe.matmul(out[:, m, :], msg[:, bu, t, at:at + P],
                                           sel[:, bu, t, :] if m < 2 else sel_ax[:, bu, t, m - 2, :], start=t == 0 and m == 0, stop=t == per - 1,
                                           skip_group_check=True)
                    mm.then_inc(s_agg, 1)

            pe.wait_ge(s_in, 48)
            pe.wait_ge(s_prep, 1)
            hidden(0, 0, 0)
            walk_groups(pe, group, GR)


def walk_groups(eng, group, n):
    group(0, 0, 0)
    with eng.Fori(0, n // 4 - 1) as i:
        for j in range(1, 5):
            group(4 * i + j, j, i)
    last = n // 4 - 1
    for j in range(1, 4):
        group(4 * last + j, j, last)
    group(None, 4, last)


def nodes_after(nc, a, K, acc, skip_table):
    with ExitStack() as ctx:
        def sb(name, shape, dt=F32):
            return ctx.enter_context(nc.sbuf_tensor(name, shape, dt))

        def sem(name):
            return ctx.enter_context(nc.semaphore(name))

        x_sb = sb("skip", [P, NODE_TILES, EMBED])
        w_sb = sb("w_fin", [P, AGG1, EMBED])
        nv = sb("nv_fin", [P, NODE_TILES])
        own = sb("own", [P, 2, AGG1, P])
        ps = [ctx.enter_context(nc.psum_tensor(f"ps_f{s}", [P, 512], F32)) for s in range(2)]
        s_x, s_w, s_scaled, s_own, s_fin, s_out = (sem("f_" + n) for n in ("x", "w", "scaled", "own", "fin", "out"))
        s_prod = [sem(f"f_prod{s}") for s in range(2)]
        block = ctx.enter_context(nc.Block())
        h = NODE_TILES // 2

        @block.sync
        def _(sp):
            sp.dma_start(w_sb[:, :, :], a["wfin"].rearrange("k p f -> p k f")).then_inc(s_w, 16)
            sp.dma_start(nv[:, :], a["nv"]).then_inc(s_w, 16)
            sp.dma_start(x_sb[:, :, :], skip_table.rearrange("(i p) f -> p i f", p=P)).then_inc(s_x, 16)
            with sp.Fori(0, h) as i:
                for s in range(2):
                    j = 2 * i + s
                    sp.wait_ge(s_fin, j + 1)
                    sp.dma_start(a["out"][bass.ds(j * P, P), :],
                                 x_sb[:, bass.ds(j, 1), :].rearrange("p a f -> p (a f)")).then_inc(s_out, 16)
            sp.wait_ge(s_out, 16 * NODE_TILES)

        @block.vector
        def _(v):
            scale = math.cos(math.pi / 8.0) / math.sqrt(2 * MUL) / math.sqrt(20.0)
            v.wait_ge(s_w, 32)
            v.tensor_scalar(w_sb[:, 0:2, :], w_sb[:, 0:2, :], scale, None, ALU.mult).then_inc(s_scaled, 1)
            for low, m, f in ((True, slice(2, 4), scale / math.sqrt(3.0)), (False, slice(2, 4), scale),
                              (True, slice(4, 5), scale), (False, slice(4, 5), scale / math.sqrt(3.0))):
                q = slice(0, MUL) if low else slice(MUL, P)
                v.tensor_scalar(w_sb[q, m, :], w_sb[q, m, :], f, None, ALU.mult).then_inc(s_scaled, 1)
            v.wait_ge(s_x, 16)
            with v.Fori(0, h) as i:
                for s in range(2):
                    j = 2 * i + s
                    row = x_sb[:, bass.ds(j, 1), :].rearrange("p a f -> p (a f)")
                    v.wait_ge(s_prod[s], i + 1)
                    v.scalar_tensor_tensor(out=row, in0=ps[s][:, 0:EMBED], scalar=nv[:, bass.ds(j, 1)], in1=row,
                                           op0=ALU.mult, op1=ALU.add).then_inc(s_fin, 1)

        @block.scalar
        def _(act):
            with act.Fori(0, h) as i:
                for s in range(2):
                    act.wait_ge(s_prod[s], i)
                    act.activation(own[:, s, :, :], acc[:, :, bass.ds((2 * i + s) * P, P)], ACT.Copy).then_inc(s_own, 1)

        @block.tensor
        def _(pe):
            pe.wait_ge(s_scaled, 5)
            with pe.Fori(0, h) as i:
                for s in range(2):
                    pe.wait_ge(s_own, 2 * i + s + 1)
                    pe.wait_ge(s_fin, 2 * i)
                    for k in range(AGG1):
                        mm = pe.matmul(ps[s][:, 0:EMBED], own[:, s, k, :], w_sb[:, k, :], start=k == 0, stop=k == AGG1 - 1)
                    mm.then_inc(s_prod[s], 1)


def kernel(**inputs):
    import numpy as np
    import concourse.bacc as bacc
    from concourse.bass_utils import run_bass_kernel_spmd

    d = {k: np.asarray(x) for k, x in inputs.items()}
    f = np.float32

    def rows(x, n, value=0):
        return np.concatenate([x, np.full((n - x.shape[0],) + x.shape[1:], value, x.dtype)])

    def by_tile(x):
        return np.ascontiguousarray(np.swapaxes(x.reshape(EDGE_TILES, P, *x.shape[1:]), 0, 1))

    src = rows(d["src"].astype(np.int32), E_PAD)
    dst = rows(d["dst"].astype(np.int32), E_PAD, N_NODES)
    ext = np.concatenate([np.full(1, -1, np.int32), dst])
    es = rows(d["edge_attr_8"], E_PAD).reshape(EDGE_TILES // 4, 2, 2, P, SCALARS)
    es = es.transpose(0, 1, 4, 2, 3).reshape(EDGE_TILES // 4, 2 * SCALARS, 2 * P)
    L0 = {n: d["L0_gnn_" + n] for n in ("Wq", "bq", "Wk", "bk", "Wv", "bv", "Wo", "bo")}
    L1 = {n: d["L1_gnn_" + n] for n in ("sc_w0", "sc_w1", "lin1_w0", "lin1_w1", "fc_w1", "fc_w2",
                                        "lin2_w00", "lin2_w01", "lin2_w10", "lin2_w11")}
    wqkv = np.concatenate([L0["Wk"].T, L0["Wv"].T, L0["Wq"].T], 1).reshape(2, P, 3 * EMBED).transpose(1, 0, 2)
    wo = np.concatenate([np.zeros((HEADS, EMBED), f), L0["Wo"].T]).reshape(AGG0, ROWS, EMBED).transpose(1, 0, 2)
    wys = np.zeros((EMBED, 2 * EMBED), f)
    wfin = np.zeros((AGG1, P, EMBED), f)
    wys[:MUL, :MUL] = L1["lin1_w0"]
    wys[:MUL, EMBED:EMBED + MUL] = L1["sc_w0"]
    wfin[0, :MUL, :MUL] = L1["lin2_w00"]
    for c in range(3):
        wys[MUL + c::3, MUL * (c + 1):MUL * (c + 2)] = L1["lin1_w1"]
        wys[MUL + c::3, EMBED + MUL + c::3] = L1["sc_w1"]
        wfin[(c + 1) // 2, ((c + 1) % 2) * MUL:((c + 1) % 2 + 1) * MUL, MUL + c::3] = L1["lin2_w11"]
        low, high = slice(0, MUL), slice(MUL, P)
        wfin[2 + c, low if c == 2 else high, MUL + c::3] = L1["lin2_w10"]
        wfin[2 + c, high if c == 2 else low, :MUL] = L1["lin2_w01"]
    wys = wys.reshape(2, P, 2 * EMBED).transpose(1, 0, 2)
    fc1 = np.zeros((2 * SCALARS, P), f)
    fc1[:SCALARS, :MUL] = fc1[SCALARS:, MUL:] = L1["fc_w1"]
    part = [L1["fc_w2"][:, MUL * k:MUL * (k + 1)] for k in (0, 3, 2, 1)]
    fc2 = np.zeros((P, 2, EMBED), f)
    fc2[:MUL, 0] = fc2[MUL:, 1] = np.concatenate(part, 1)
    place = np.zeros((HEADS, AGG0 * ROWS), f)
    for h in range(HEADS):
        place[h, h] = 1.0
        place[h, HEADS + h * HDIM:HEADS + (h + 1) * HDIM] = 1.0
    arrays = {
        "x": rows(d["x"], N_PAD),
        "src_line": src.reshape(CHUNKS, TILES, P).transpose(0, 2, 1),
        "dst_tile": by_tile(dst),
        "dst_line": np.lib.stride_tricks.sliding_window_view(ext, CHUNK + 1)[::CHUNK],
        "first": dst[None, ::P],
        "fold": np.tile(np.eye(MUL, dtype=f), (2, 1)),
        "ident": np.eye(P, dtype=f),
        "iota": np.arange(P, dtype=f)[None],
        "part": np.arange(P, dtype=f)[:, None],
        "place": place.reshape(HEADS, AGG0, ROWS),
        "wqkv": wqkv, "bqkv": np.concatenate([L0["bk"], L0["bv"], L0["bq"]])[None],
        "wo": wo, "bo": L0["bo"][None], "wys": wys, "wfin": wfin, "fc1": fc1, "fc2": fc2,
        "nv": rows(d["node_vec1"], N_PAD)[:, 0].reshape(NODE_TILES, P).T,
        "ea": by_tile(rows(d["edge_attr_4"], E_PAD)),
        "es": es,
    }
    nc = bacc.Bacc("TRN2", target_bir_lowering=False, num_devices=1)
    aps, feed = {}, {}
    for n, x in arrays.items():
        x = np.ascontiguousarray(x)
        feed["in_" + n] = x
        aps[n] = nc.dram_tensor("in_" + n, x.shape, mybir.dt.from_np(x.dtype), kind="ExternalInput").ap()
    aps["out"] = nc.dram_tensor("out", (N_PAD, EMBED), F32, kind="ExternalOutput").ap()
    build(nc, aps)
    r = run_bass_kernel_spmd(nc, [feed], core_ids=[0])
    return r.results[0]["out"][:N_NODES]
```

```python
import math
from contextlib import ExitStack

import concourse.bass as bass
from concourse import mybir

F32 = mybir.dt.float32
BF16 = mybir.dt.bfloat16
I32 = mybir.dt.int32
U32 = mybir.dt.uint32
ALU = mybir.AluOpType
ACT = mybir.ActivationFunctionType
AX_X = mybir.AxisListType.X

P = 128
N_NODES = 6250
N_EDGES = 106250
EMBED = 256
HEADS = 8
HDIM = EMBED // HEADS
MUL = 64
SCALARS = 8
EPS = 1e-5
TILES = 8
CHUNK = TILES * P
CHUNKS = -(-N_EDGES // CHUNK)
EDGE_TILES = CHUNKS * TILES
E_PAD = CHUNKS * CHUNK
NODE_TILES = 2 * (-(-(N_NODES + P) // (2 * P)))
N_PAD = NODE_TILES * P
HALF = TILES // 2
ROWS = 88
AGG0 = 3
MSG = HEADS + EMBED
AGG1 = 5
CONV_TILES = 4
CHUNK_NODES = 80
CONV_NODES = 38
NEG = -1e30
UNROLL = 4


def build(nc, a):
    with ExitStack() as whole:
        s_turn = [whole.enter_context(nc.semaphore(f"s_turn_{e}")) for e in ("pool", "pe")]
        kv_table = nc.dram_tensor("kv_table", [N_PAD, 2 * EMBED], F32).ap()
        q_table = nc.dram_tensor("q_table", [N_PAD, EMBED], F32).ap()
        y_table = nc.dram_tensor("y_table", [N_PAD, EMBED], F32).ap()
        skip_table = nc.dram_tensor("skip_table", [N_PAD, EMBED], F32).ap()
        dst_rows = nc.dram_tensor("dst_rows", [CHUNKS, CHUNK // 2], F32).ap()
        near_rows = nc.dram_tensor("near_rows", [CHUNKS, CHUNK // 2], F32).ap()
        new_rows = nc.dram_tensor("new_rows", [CHUNKS, CHUNK // 2], F32).ap()
        K = Constants(nc, whole)
        K.turn_pe = s_turn[1]
        with ExitStack() as zero:
            tables = Tables(nc, zero, a, K, dst_rows, near_rows, new_rows)
            nodes_before_attention(nc, a, K, tables, kv_table, q_table)
        with ExitStack() as one:
            acc = one.enter_context(nc.sbuf_tensor("attn_sum", [P, AGG0, N_PAD], F32))
            signals = AttentionSignals(nc, one)
            places = [one.enter_context(nc.semaphore(n)) for n in ("s_places_in", "s_places")]
            wide = nc.values_load(K.wide[0:1, 0:1], min_val=0, max_val=1)
            with nc.If(wide < 1):
                attention_edges(nc, a, K, acc, kv_table, q_table, dst_rows, new_rows, s_turn, signals,
                                TILES, CHUNK_NODES, 4)
            with nc.Else():
                window_places(nc, a, K, 1, "attn", *places)
                attention_edges(nc, a, K, acc, kv_table, q_table, near_rows, new_rows, s_turn, signals, 1, P, 2)
            nodes_between(nc, a, K, acc, y_table, skip_table)
        with ExitStack() as two:
            acc = two.enter_context(nc.sbuf_tensor("conv_sum", [P, AGG1, N_PAD], F32))
            signals = ConvolutionSignals(nc, two)
            places = [two.enter_context(nc.semaphore(n)) for n in ("s_wide_in", "s_wide")]
            wide = nc.values_load(K.wide[0:1, 1:2], min_val=0, max_val=1)
            with nc.If(wide < 1):
                convolution_edges(nc, a, K, acc, y_table, s_turn, signals, False)
            with nc.Else():
                window_places(nc, a, K, 1, "wide", *places)
                convolution_edges(nc, a, K, acc, y_table, s_turn, signals, True)
            nodes_after(nc, a, K, acc, skip_table)


class Constants:

    def __init__(self, nc, ctx):
        def sb(name, shape, dt=F32):
            return ctx.enter_context(nc.sbuf_tensor(name, shape, dt))

        self.ident = sb("ident", [P, P])
        self.iota = sb("iota", [P, P])
        self.wide = sb("wide", [1, 2], I32)
        self.place = sb("place", [P, AGG0, P])
        self.dst_rel = sb("dst_rel", [P, EDGE_TILES])
        self.part = sb("part", [P, 1])
        self.first = sb("first", [1, EDGE_TILES], I32)


class Count:

    def __init__(self, eng, sem):
        self.eng, self.sem, self.n = eng, sem, 0

    def __call__(self, ins):
        self.n += 1
        ins.then_inc(self.sem, 1)
        self.eng.wait_ge(self.sem, self.n)


def rounds(eng, n, body):
    body(0)
    with eng.Fori(1, n) as i:
        body(i)


def wait_then(eng, sem, value, turn):
    eng.wait_ge(sem, value)
    eng.sem_inc(turn, 1)


class Tables:

    def __init__(self, nc, ctx, a, K, dst_rows, near_rows, new_rows):
        def sb(name, shape, dt=F32):
            return ctx.enter_context(nc.sbuf_tensor(name, shape, dt))

        self.a, self.K = a, K
        self.dst_rows, self.near_rows, self.new_rows = dst_rows, near_rows, new_rows
        self.lin_i = sb("lin_i", [CHUNKS, CHUNK + 1], I32)
        self.lin = sb("lin", [CHUNKS, CHUNK + 1])
        self.rel = sb("rel", [CHUNKS, CHUNK], BF16)
        self.near = sb("near", [CHUNKS, CHUNK], BF16)
        self.new = sb("new_line", [CHUNKS, CHUNK], BF16)
        self.ends = sb("ends", [1, 2, EDGE_TILES], I32)
        self.ends_f = sb("ends_f", [1, 2, EDGE_TILES])
        self.span = sb("span", [1, EDGE_TILES])
        self.widest = sb("widest", [1, 2])
        self.s_in, self.s_v, self.s_out = (ctx.enter_context(nc.semaphore(n))
                                           for n in ("s_in", "s_prep", "s_prep_out"))

    def load(self, sp):
        K, a = self.K, self.a
        for dst, src in ((self.ends[:, 0, :], a["first"]), (self.ends[:, 1, :], a["last"]),
                         (self.lin_i[:, :], a["dst_line"]), (K.ident[:, :], a["ident"]),
                         (K.iota[:, :], a["iota"].to_broadcast([P, P])), (K.place[:, :, :], a["place"]),
                         (K.first[:, :], a["first"]), (K.part[:, :], a["part"])):
            sp.dma_start(dst, src).then_inc(self.s_in, 16)

    def store(self, sp):
        sp.wait_ge(self.s_v, 5)
        for dst, src in ((self.dst_rows, self.rel), (self.new_rows, self.new), (self.near_rows, self.near)):
            sp.dma_start(dst, src[:, :].bitcast(F32)).then_inc(self.s_out, 16)

    def work_out(self, v):
        K, lin, rel, near, new, span = self.K, self.lin, self.rel, self.near, self.new, self.span
        step = Count(v, self.s_v)
        v.wait_ge(self.s_in, 16 * 8)
        step(v.tensor_copy(lin[:, :], self.lin_i[:, :]))
        step(v.tensor_scalar(rel[:, :], lin[:, 1:CHUNK + 1], lin[:, 1:2], None, ALU.subtract))
        step(v.tensor_tensor(near[:, :].rearrange("c (t e) -> c t e", e=P),
                             lin[:, 1:CHUNK + 1].rearrange("c (t e) -> c t e", e=P),
                             lin[:, 1:CHUNK:P].unsqueeze(2).to_broadcast([CHUNKS, TILES, P]), ALU.subtract))
        step(v.tensor_tensor(new[:, :], lin[:, 1:CHUNK + 1], lin[:, 0:CHUNK], ALU.not_equal))
        step(v.tensor_scalar(new[:, :], new[:, :], NEG, None, ALU.mult))
        step(v.tensor_copy(self.ends_f[:, :, :], self.ends[:, :, :]))
        for n, (per, W) in enumerate(((TILES, CHUNK_NODES), (CONV_TILES, CONV_NODES))):
            step(v.tensor_tensor(span[:, 0:EDGE_TILES // per], self.ends_f[:, 1, per - 1::per],
                                 self.ends_f[:, 0, 0::per], ALU.subtract))
            step(v.tensor_reduce(self.widest[:, n:n + 1], span[:, 0:EDGE_TILES // per], AX_X, ALU.max))
            step(v.tensor_scalar(K.wide[:, n:n + 1], self.widest[:, n:n + 1], float(W), None, ALU.is_ge))


class WindowPlaces:

    def __init__(self, nc, ctx, a, K, name, s_in, s_v):
        self.a, self.K, self.s_in, self.s_v = a, K, s_in, s_v
        self.dst_t = ctx.enter_context(nc.sbuf_tensor(f"dst_t_{name}", [P, EDGE_TILES], I32))
        self.first_t = ctx.enter_context(nc.sbuf_tensor(f"first_t_{name}", [P, EDGE_TILES], I32))
        self.first_f = ctx.enter_context(nc.sbuf_tensor(f"first_f_{name}", [P, EDGE_TILES], F32))

    def load(self, sp):
        sp.dma_start(self.first_t[:, :], self.a["first"].to_broadcast([P, EDGE_TILES])).then_inc(self.s_in, 16)
        sp.dma_start(self.dst_t[:, :], self.a["dst_tile"]).then_inc(self.s_in, 16)

    def work_out(self, v, per):
        step = Count(v, self.s_v)
        v.wait_ge(self.s_in, 32)
        step(v.tensor_copy(self.first_f[:, :], self.first_t[:, :]))
        step(v.tensor_tensor(self.K.dst_rel[:, :].rearrange("p (g t) -> p g t", t=per),
                             self.dst_t[:, :].rearrange("p (g t) -> p g t", t=per),
                             self.first_f[:, 0:EDGE_TILES:per].unsqueeze(2).to_broadcast([P, EDGE_TILES // per, per]),
                             ALU.subtract))


def window_places(nc, a, K, per, name, s_in, s_v):
    with ExitStack() as ctx:
        places = WindowPlaces(nc, ctx, a, K, name, s_in, s_v)
        block = ctx.enter_context(nc.Block())

        @block.sync
        def _(sp):
            places.load(sp)

        @block.vector
        def _(v):
            places.work_out(v, per)


def layer_stats(v, stats, mean, rstd, tmp, step):
    cnt = EMBED
    me, mo = stats[:, :, 1], stats[:, :, 4]
    step(v.tensor_tensor(mean[:, :], me, mo, ALU.add))
    step(v.tensor_scalar(mean[:, :], mean[:, :], 0.5, None, ALU.mult))
    step(v.tensor_tensor(tmp[:, :], me, mo, ALU.subtract))
    step(v.tensor_tensor(tmp[:, :], tmp[:, :], tmp[:, :], ALU.mult))
    step(v.tensor_tensor(rstd[:, :], stats[:, :, 2], stats[:, :, 5], ALU.add))
    step(v.tensor_scalar(rstd[:, :], rstd[:, :], 1.0 / cnt, EPS, ALU.mult, ALU.add))
    step(v.scalar_tensor_tensor(out=rstd[:, :], in0=tmp[:, :], scalar=0.25, in1=rstd[:, :],
                                op0=ALU.mult, op1=ALU.add))



class NodePass:

    def __init__(self, nc, ctx, name, K, x_sb, w_sb, width):
        def sb(n, shape):
            return ctx.enter_context(nc.sbuf_tensor(f"{name}_{n}", shape, F32))

        def sem(n):
            return ctx.enter_context(nc.semaphore(f"{name}_{n}"))

        self.K, self.x_sb, self.w_sb, self.width = K, x_sb, w_sb, width
        self.h = sb("h", [P, 2, EMBED])
        self.hT = sb("hT", [P, 2, 2, P])
        self.stats = sb("stats", [P, NODE_TILES, 6])
        self.shift, self.scale, self.tmp = (sb(n, [P, NODE_TILES]) for n in ("shift", "scale", "tmp"))
        self.ps_t = [ctx.enter_context(nc.psum_tensor(f"{name}_turned{i}", [P, 2, P], F32)) for i in range(2)]
        self.ps_m = [ctx.enter_context(nc.psum_tensor(f"{name}_prod{i}", [P, 512 * -(-width // 512)], F32))
                     for i in range(2)]
        self.s_step, self.s_var, self.s_root, self.s_norm = sem("step"), sem("var"), sem("root"), sem("norm")
        self.s_stat, self.s_h, self.s_turned, self.s_copied = (
            sem(n) for n in ("s_stat", "s_h", "s_turned", "s_copied"))
        self.s_prod = [sem(f"s_prod{i}") for i in range(2)]
        self.s_taken = [sem(f"s_taken{i}") for i in range(2)]

    def row_stats(self, v, j):
        v.bn_stats(self.stats[:, bass.ds(j, 1), :].rearrange("p a s -> p (a s)"),
                   self.x_sb[:, bass.ds(j, 1), :].rearrange("p a s -> p (a s)")).then_inc(self.s_stat, 1)

    def statistics(self, v, step):
        v.wait_ge(self.s_stat, NODE_TILES)
        layer_stats(v, self.stats, self.shift, self.scale, self.tmp, step)
        v.sem_inc(self.s_var, 1)
        v.wait_ge(self.s_root, 1)
        step(v.reciprocal(self.scale[:, :], self.scale[:, :]))
        step(v.scalar_tensor_tensor(out=self.shift[:, :], in0=self.shift[:, :], scalar=-1.0,
                                    in1=self.scale[:, :], op0=ALU.mult, op1=ALU.mult))
        v.sem_inc(self.s_norm, 1)

    def scalar(self, act):
        act.wait_ge(self.s_var, 1)
        act.activation(self.scale[:, :], self.scale[:, :], ACT.Sqrt).then_inc(self.s_root, 1)
        act.wait_ge(self.s_norm, 1)

        def relu(j, s):
            act.activation(self.h[:, s, :], self.x_sb[:, bass.ds(j, 1), :].rearrange("p a f -> p (a f)"),
                           ACT.Relu, bias=self.shift[:, bass.ds(j, 1)],
                           scale=self.scale[:, bass.ds(j, 1)]).then_inc(self.s_h, 1)

        def copy(j, s, rounds):
            act.wait_ge(self.s_turned, j + 1)
            act.wait_ge(self.s_prod[s], rounds)
            act.activation(self.hT[:, s, :, :], self.ps_t[s][:, :, :], ACT.Copy).then_inc(self.s_copied, 1)

        relu(0, 0)
        def both(i):
            for s in range(2):
                act.wait_ge(self.s_turned, 2 * i + s)
                relu(2 * i + s + 1, 1 - s)
                copy(2 * i + s, s, i)

        rounds(act, NODE_TILES // 2 - 1, both)
        last = NODE_TILES - 2
        act.wait_ge(self.s_turned, last)
        relu(last + 1, 1)
        copy(last, 0, last // 2)
        copy(last + 1, 1, last // 2)

    def tensor(self, pe):
        def turn(j, s):
            pe.wait_ge(self.s_h, j + 1)
            for c in range(2):
                mm = pe.transpose(self.ps_t[s][:, c, :], self.h[:, s, c * P:(c + 1) * P], self.K.ident[:, :])
            mm.then_inc(self.s_turned, 1)

        def project(j, s, rounds):
            pe.wait_ge(self.s_copied, j + 1)
            pe.wait_ge(self.s_taken[s], rounds)
            for n in range(0, self.width, 512):
                m = min(self.width, n + 512)
                for c in range(2):
                    mm = pe.matmul(self.ps_m[s][:, n:m], self.hT[:, s, c, :], self.w_sb[:, c, n:m],
                                   start=c == 0, stop=c == 1)
            mm.then_inc(self.s_prod[s], 1)

        turn(0, 0)
        def both(i):
            for s in range(2):
                turn(2 * i + s + 1, 1 - s)
                project(2 * i + s, s, i)

        rounds(pe, NODE_TILES // 2 - 1, both)
        last = NODE_TILES - 2
        turn(last + 1, 1)
        project(last, 0, last // 2)
        project(last + 1, 1, last // 2)


def nodes_before_attention(nc, a, K, tables, kv_table, q_table):
    WID = 3 * EMBED
    with ExitStack() as ctx:
        def sb(name, shape, dt=F32):
            return ctx.enter_context(nc.sbuf_tensor(name, shape, dt))

        def sem(name):
            return ctx.enter_context(nc.semaphore(name))

        x_sb = sb("x_sb", [P, NODE_TILES, EMBED])
        w_sb = sb("w_sb", [P, 2, WID])
        b_sb = sb("b_sb", [P, WID])
        o_sb = sb("o_sb", [P, 2, WID])
        N = NodePass(nc, ctx, "pre", K, x_sb, w_sb, WID)
        PIECES = 5
        s_w, s_scaled = sem("s_w"), sem("s_scaled")
        places = WindowPlaces(nc, ctx, a, K, "pre", sem("s_places_in"), sem("s_places"))
        s_x = [sem(f"s_x{q}") for q in range(PIECES)]
        s_stored = [sem(f"s_stored{i}") for i in range(2)]
        block = ctx.enter_context(nc.Block())
        x_d = a["x"].rearrange("(i p) f -> p i f", p=P)
        h = NODE_TILES // 2
        n = NODE_TILES // PIECES

        @block.sync
        def _(sp):
            for q in range(PIECES):
                sp.dma_start(x_sb[:, q * n:(q + 1) * n, :], x_d[:, q * n:(q + 1) * n, :]).then_inc(s_x[q], 16)
                if q == 0:
                    tables.load(sp)
                    places.load(sp)
                    sp.dma_start(w_sb[:, :, :], a["wqkv"]).then_inc(s_w, 16)
                    sp.dma_start(b_sb[:, :], a["bqkv"].to_broadcast([P, WID])).then_inc(s_w, 16)
            tables.store(sp)
            def both(i):
                for s in range(2):
                    sp.wait_ge(N.s_taken[s], i + 1)
                    row = bass.ds((2 * i + s) * P, P)
                    sp.dma_start(kv_table[row, :], o_sb[:, s, 0:2 * EMBED]).then_inc(s_stored[s], 16)
                    sp.dma_start(q_table[row, :], o_sb[:, s, 2 * EMBED:WID]).then_inc(s_stored[s], 16)

            rounds(sp, h, both)
            for s in range(2):
                sp.wait_ge(s_stored[s], 32 * h)
            sp.wait_ge(tables.s_out, 48)

        @block.vector
        def _(v):
            step = Count(v, N.s_step)
            tables.work_out(v)
            places.work_out(v, TILES)
            v.wait_ge(s_w, 32)
            step(v.tensor_scalar(w_sb[:, :, 2 * EMBED:WID], w_sb[:, :, 2 * EMBED:WID], HDIM ** -0.5, None, ALU.mult))
            step(v.tensor_scalar(b_sb[:, 2 * EMBED:WID], b_sb[:, 2 * EMBED:WID], HDIM ** -0.5, None, ALU.mult))
            v.sem_inc(s_scaled, 1)
            for q in range(PIECES):
                v.wait_ge(s_x[q], 16)
                with v.Fori(q * n, (q + 1) * n) as i:
                    N.row_stats(v, i)
            N.statistics(v, step)
            def both(i):
                for s in range(2):
                    v.wait_ge(N.s_prod[s], i + 1)
                    v.wait_ge(s_stored[s], 32 * i)
                    v.tensor_tensor(o_sb[:, s, :], N.ps_m[s][:, 0:WID], b_sb[:, :],
                                    ALU.add).then_inc(N.s_taken[s], 1)

            rounds(v, h, both)

        @block.scalar
        def _(act):
            N.scalar(act)

        @block.tensor
        def _(pe):
            pe.wait_ge(s_scaled, 1)
            N.tensor(pe)


class AttentionSignals:

    def __init__(self, nc, ctx):
        def sem(*names):
            return [ctx.enter_context(nc.semaphore("s_" + n)) for n in names]

        def slots(name, n):
            return sem(*(f"{name}{i}" for i in range(n)))

        self.idx, self.kv, self.kv_used = slots("idx", 4), slots("kv", 4), slots("kv_used", 4)
        self.rows, self.rows_used = slots("rows", 2), slots("rows_used", 2)
        self.new, self.new_used = slots("new", 2), slots("new_used", 2)
        self.zero, self.blank = sem("zero", "blank")
        self.farT, self.selT, self.far, self.sel = sem("farT", "selT", "far", "sel")
        self.q, self.mul, self.score, self.scoreT = sem("q", "mul", "score", "scoreT")
        self.run, self.top, self.topT, self.diff, self.exp = sem("run", "top", "topT", "diff", "exp")
        self.fall, self.fade, self.fadeR, self.faded = sem("fall", "fade", "fadeR", "faded")
        self.msg, self.part, self.kept, self.agg, self.sum = sem("msg", "part", "kept", "agg", "sum")


def attention_edges(nc, a, K, acc, kv_table, q_table, dst_rows, new_rows, s_turn, S, per, W, R):
    GR = TILES // per
    QW = 1 if GR == 1 else TILES
    ROWS_IN = 16 * (1 + QW)
    turn_pool, turn_pe = s_turn
    with ExitStack() as ctx:
        def sb(name, shape, dt=F32):
            return ctx.enter_context(nc.sbuf_tensor(f"{name}_{per}", shape, dt))

        def psum(name, shape):
            return ctx.enter_context(nc.psum_tensor(f"{name}_{per}", shape, F32))

        kv = sb("kv", [P, R, TILES, 2 * EMBED])
        idx = sb("idx", [P, R, TILES], I32)
        rows = sb("rows", [P, 2, CHUNK], BF16)
        new = sb("new", [HEADS, 2, CHUNK], BF16)
        qw = sb("qw", [P, 2, QW, EMBED])
        sel = sb("sel", [P, 2, TILES, P])
        selT = sb("selT", [P, CHUNK])
        prod = sb("prod", [P, 2, HALF, EMBED])
        score = sb("score", [P, 2, TILES * HEADS])
        top = sb("top", [HEADS, 2, CHUNK])
        diff = sb("diff", [P, TILES * HEADS])
        msg = sb("msg", [P, 2, TILES, MSG])
        fall = sb("fall", [HEADS, 1])
        fade = sb("fade", [HEADS, 1])
        ps_q = [psum(f"ps_q{h}", [P, HALF, EMBED]) for h in range(2)]
        ps_s = psum("ps_s", [P, CHUNK])
        part = sb("part_sums", [P, MSG])
        ps_p = psum("ps_p", [P, 512])
        ps_a = psum("ps_a", [P, 512])
        turned = ps_a[0:ROWS, 0:AGG0 * W].rearrange("p (k w) -> p k w", w=W)
        ps_top = ps_s[:, 0:TILES * HEADS]
        ps_fade = ps_a[0:ROWS, 448:448 + AGG0]

        block = ctx.enter_context(nc.Block())
        U = UNROLL
        src_d = a["src_line"]

        @block.sync
        def _(sp):
            def chunks(i):
                for m in range(U):
                    c, r, u, k = U * i + m, m % R, m % 2, i * (U // 2) + m // 2
                    n0 = [sp.value_load(K.first[0:1, bass.ds(c * TILES + w, 1)], min_val=0, max_val=N_NODES)
                          for w in range(QW)]
                    sp.wait_ge(S.kv[r], (i * (U // R) + m // R) * 16 * TILES)
                    sp.dma_start(idx[:, r, :], src_d[bass.ds(c, 1), :, :].rearrange("a p t -> p (a t)")
                                 ).then_inc(S.idx[r], 16)
                    sp.wait_ge(S.rows_used[u], k)
                    row = bass.ds(c, 1)
                    sp.dma_start(rows[:, u, :].bitcast(F32), dst_rows[row, :].to_broadcast([P, CHUNK // 2])).then_inc(S.rows[u], 16)
                    for w in range(QW):
                        sp.dma_start(qw[:, u, w, :], q_table[bass.ds(n0[w], P), :]).then_inc(S.rows[u], 16)
                    sp.wait_ge(S.new_used[u], k)
                    sp.dma_start(new[:, u, :].bitcast(F32), new_rows[row, :].to_broadcast([HEADS, CHUNK // 2])).then_inc(S.new[u], 16)

            rounds(sp, CHUNKS // U, chunks)

        @block.gpsimd
        def _(gp):
            def chunks(i):
                for m in range(U):
                    r, k = m % R, i * (U // R) + m // R
                    wait_then(gp, S.idx[r], 16 * (k + 1), turn_pool)
                    wait_then(gp, S.kv_used[r], k, turn_pool)
                    for t in range(TILES):
                        gp.indirect_dma_start(kv[:, r, t, :], None, kv_table,
                                              bass.IndirectOffsetOnAxis(ap=idx[:, r, t:t + 1].bitcast(U32), axis=0)
                                              ).then_inc(S.kv[r], 16)

            rounds(gp, CHUNKS // U, chunks)

        @block.vector
        def _(v):
            v.memset(acc[:, 0, :], 0.0).then_inc(S.zero, 1)
            v.wait_ge(S.zero, 1)
            v.memset(acc[0:HEADS, 0, :], 1e-15).then_inc(S.zero, 1)
            v.memset(top[:, 1, CHUNK - 1:CHUNK], NEG).then_inc(S.zero, 1)
            v.wait_ge(S.zero, 3)
            v.wait_ge(S.blank, 3)

            def multiply(c, r, k):
                v.wait_ge(S.kv[r], 16 * TILES * (k + 1))
                for h in range(2):
                    v.wait_ge(S.q, 2 * c + h + 1)
                    v.tensor_tensor(prod[:, h, :, :], kv[:, r, h * HALF:(h + 1) * HALF, 0:EMBED],
                                    ps_q[h][:, :, :], ALU.mult).then_inc(S.mul, 1)

            def add_up(c, h, u):
                v.wait_ge(S.mul, 2 * c + h + 1)
                v.tensor_reduce(score[:, u, h * HALF * HEADS:(h + 1) * HALF * HEADS],
                                prod[:, h, :, :].rearrange("p t (h d) -> p (t h) d", d=HDIM),
                                AX_X, ALU.add).then_inc(S.score, 1)

            def weigh(c, u):
                v.wait_ge(S.topT, c + 1)
                v.wait_ge(S.exp, c)
                v.tensor_tensor(diff[:, :], score[:, u, :], ps_top, ALU.subtract).then_inc(S.diff, 1)

            def run(c, u, k):
                v.wait_ge(S.scoreT, c + 1)
                v.wait_ge(S.new[u], 16 * (k + 1))
                v.wait_ge(S.top, c)
                v.tensor_tensor_scan(top[:, u, :], new[:, u, :], ps_s[0:HEADS, :], top[:, 1 - u, CHUNK - 1:CHUNK],
                                     ALU.add, ALU.max).then_inc(S.run, 1)

            def spread(c, u):
                v.wait_ge(S.run, c + 1)
                v.tensor_tensor_scan(top[:, u, CHUNK - 2::-1], new[:, u, CHUNK - 1:0:-1], top[:, u, CHUNK - 2::-1],
                                     top[:, u, CHUNK - 1:CHUNK], ALU.add, ALU.max).then_inc(S.top, 1)

            def rise(c, u):
                v.wait_ge(S.top, c + 1)
                v.wait_ge(S.fade, c)
                v.tensor_scalar(fall[:, :], top[:, 1 - u, CHUNK - 1:CHUNK], top[:, u, 0:1], 0.0,
                                ALU.subtract, ALU.min).then_inc(S.fall, 1)
                v.sem_inc(S.new_used[u], 1)

            def messages(c, h, r, u):
                v.wait_ge(S.exp, c + 1)
                t = slice(h * HALF, (h + 1) * HALF)
                v.tensor_tensor(msg[:, u, t, HEADS:MSG].rearrange("p t (h d) -> p t h d", d=HDIM),
                                kv[:, r, t, EMBED:2 * EMBED].rearrange("p t (h d) -> p t h d", d=HDIM),
                                msg[:, u, t, 0:HEADS].unsqueeze(3).to_broadcast([P, HALF, HEADS, HDIM]),
                                ALU.mult).then_inc(S.msg, 1)

            def first(c, g):
                return v.value_load(K.first[0:1, bass.ds(c * TILES + g * per, 1)], min_val=0, max_val=N_NODES)

            def fade_sums(c):
                n0 = first(c, 0)
                v.wait_ge(S.fadeR, c + 1)
                v.wait_ge(S.sum, GR * c)
                v.tensor_tensor(acc[0:ROWS, :, bass.ds(n0, 1)], acc[0:ROWS, :, bass.ds(n0, 1)], ps_fade.unsqueeze(2),
                                ALU.mult).then_inc(S.faded, 1)
                v.wait_ge(S.faded, c + 1)

            def sums(c, g):
                n0 = first(c, g)
                v.wait_ge(S.agg, GR * c + g + 1)
                v.wait_ge(S.sum, GR * c + g)
                v.tensor_tensor(acc[0:ROWS, :, bass.ds(n0, W)], acc[0:ROWS, :, bass.ds(n0, W)], turned,
                                ALU.add).then_inc(S.sum, 1)

            def chunk(c, j, i):
                u, now, past, older = j % 2, exists(c), exists(c - 1), exists(c - 2)
                if past:
                    rise(c - 1, 1 - u)
                    weigh(c - 1, 1 - u)
                if older:
                    v.wait_ge(S.msg, 2 * (c - 1))
                    v.sem_inc(S.kv_used[(j - 2) % R], 1)
                if now:
                    multiply(c, j % R, i * (U // R) + j // R)
                if now:
                    add_up(c, 0, u)
                    add_up(c, 1, u)
                if older:
                    for g in range(GR - 1):
                        sums(c - 2, g)
                if past:
                    messages(c - 1, 0, (j - 1) % R, 1 - u)
                if now:
                    run(c, u, i * (U // 2) + j // 2)
                if older:
                    sums(c - 2, GR - 1)
                if now:
                    spread(c, u)
                if past:
                    fade_sums(c - 1)
                    messages(c - 1, 1, (j - 1) % R, 1 - u)

            walk(v, chunk, CHUNKS, 2)

        @block.scalar
        def _(act):
            def select_turned(c, u, k):
                act.wait_ge(S.rows[u], ROWS_IN * (k + 1))
                act.wait_ge(S.q, 2 * c)
                act.activation(selT[:, :], rows[:, u, :], ACT.Square, scale=-1.0, bias=K.part[:, 0:1]).then_inc(S.farT, 1)
                act.wait_ge(S.farT, c + 1)
                act.activation(selT[:, :], selT[:, :], ACT.Relu, scale=-1.0, bias=1.0).then_inc(S.selT, 1)

            def clear(k):
                act.activation(acc[:, k, :], K.ident[:, 0:1].to_broadcast([P, N_PAD]), ACT.Copy,
                               scale=0.0).then_inc(S.blank, 1)

            def select(c, u):
                if exists(c - 2):
                    act.wait_ge(S.part, GR * (c - 1))
                for t in range(TILES):
                    ins = act.activation(sel[:, u, t, 0:W], K.iota[:, 0:W], ACT.Square, scale=-1.0,
                                         bias=K.dst_rel[:, bass.ds(c * TILES + t, 1)])
                ins.then_inc(S.far, 1)
                act.wait_ge(S.far, c + 1)
                act.activation(sel[:, u, :, 0:W], sel[:, u, :, 0:W], ACT.Relu, scale=-1.0, bias=1.0).then_inc(S.sel, 1)

            def chunk(c, j, i):
                if j == 0 and c == 0:
                    select_turned(0, 0, 0)
                if exists(c - 1):
                    act.wait_ge(S.fall, c)
                    act.wait_ge(S.fadeR, c - 1)
                    act.activation(fade[:, :], fall[:, :], ACT.Exp).then_inc(S.fade, 1)
                    act.wait_ge(S.diff, c)
                    if exists(c - 3):
                        act.wait_ge(S.part, GR * (c - 2))
                    act.activation(msg[:, (j - 1) % 2, :, 0:HEADS], diff[:, :].rearrange("p (t h) -> p t h", h=HEADS),
                                   ACT.Exp).then_inc(S.exp, 1)
                if exists(c + 1):
                    select_turned(c + 1, (j + 1) % 2, i * (U // 2) + (j + 1) // 2)
                if exists(c - 2):
                    for g in range(GR):
                        act.wait_ge(S.part, GR * (c - 2) + g + 1)
                        if exists(c - 3) or g > 0:
                            act.wait_ge(S.agg, GR * (c - 2) + g)
                        act.activation(part[:, :], ps_p[:, 0:MSG], ACT.Copy).then_inc(S.kept, 1)

                if exists(c - 1):
                    select(c - 1, (j - 1) % 2)

            clear(1)
            clear(2)
            act.activation(sel[:, :, :, :], K.ident[:, 0:1].to_broadcast([P, 2 * TILES * P]).rearrange(
                "p (u t w) -> p u t w", u=2, t=TILES), ACT.Copy, scale=0.0).then_inc(S.blank, 1)
            act.wait_ge(S.blank, 3)
            walk(act, chunk, CHUNKS, 2)

        @block.tensor
        def _(pe):
            def queries(c, h, u, k):
                pe.wait_ge(S.rows[u], ROWS_IN * (k + 1))
                pe.wait_ge(S.selT, c + 1)
                if not isinstance(c, int) or c > 0:
                    pe.wait_ge(S.mul, 2 * c - 1 + h)
                for t in range(HALF):
                    tile = h * HALF + t
                    mm = pe.matmul(ps_q[h][:, t, :], selT[:, tile * P:(tile + 1) * P],
                                   qw[:, u, tile if QW > 1 else 0, :], start=True, stop=True)
                mm.then_inc(S.q, 1)

            def sums(c, g, u):
                pe.wait_ge(S.msg, 2 * c + 2)
                pe.wait_ge(S.sel, c + 1)
                pe.wait_ge(S.kept, GR * c + g)
                for t in range(per):
                    mm = pe.matmul(ps_p[:, 0:MSG], sel[:, u, g * per + t, :], msg[:, u, g * per + t, :],
                                   start=t == 0, stop=t == per - 1)
                mm.then_inc(S.part, 1)

            def turn_sums(c, g):
                pe.wait_ge(S.kept, GR * c + g + 1)
                pe.wait_ge(S.sum, GR * c + g)
                if g == 0:
                    pe.wait_ge(S.faded, c + 1)
                for m in range(AGG0):
                    mm = pe.matmul(turned[:, m, :], part[:, m * ROWS:(m + 1) * ROWS], K.ident[:, 0:W],
                                   start=True, stop=True)
                mm.then_inc(S.agg, 1)

            def turn_scores(c, u):
                pe.wait_ge(S.score, 2 * c + 2)
                pe.wait_ge(S.diff, c)
                for t in range(TILES):
                    mm = pe.transpose(ps_s[0:HEADS, t * P:(t + 1) * P],
                                      score[:, u, t * HEADS:(t + 1) * HEADS], K.ident[:, :])
                mm.then_inc(S.scoreT, 1)

            def turn_top(c, u):
                wait_then(pe, S.top, c + 1, turn_pe)
                for t in range(TILES):
                    mm = pe.transpose(ps_top[:, t * HEADS:(t + 1) * HEADS], top[:, u, t * P:(t + 1) * P],
                                      K.ident[0:HEADS, 0:HEADS])
                mm.then_inc(S.topT, 1)

            def spread_fade(c):
                wait_then(pe, S.faded, c, turn_pe)
                wait_then(pe, S.fade, c + 1, turn_pe)
                for m in range(AGG0):
                    mm = pe.matmul(ps_fade[:, m:m + 1], K.place[0:HEADS, m, 0:ROWS], fade[:, :], start=True, stop=True)
                mm.then_inc(S.fadeR, 1)

            def chunk(c, j, i):
                if j == 0 and c == 0:
                    queries(0, 0, 0, 0)
                if exists(c - 1):
                    turn_top(c - 1, (j - 1) % 2)
                if exists(c):
                    queries(c, 1, j % 2, i * (U // 2) + j // 2)
                if exists(c - 2):
                    sums(c - 2, 0, j % 2)
                if exists(c):
                    wait_then(pe, S.q, 2 * c + 2, turn_pe)
                    pe.sem_inc(S.rows_used[j % 2], 1)
                if exists(c - 1):
                    spread_fade(c - 1)
                if exists(c - 2):
                    for g in range(1, GR):
                        turn_sums(c - 2, g - 1)
                        sums(c - 2, g, j % 2)
                if exists(c):
                    turn_scores(c, j % 2)
                if exists(c - 2):
                    turn_sums(c - 2, GR - 1)
                if exists(c + 1):
                    queries(c + 1, 0, (j + 1) % 2, i * (U // 2) + (j + 1) // 2)

            walk(pe, chunk, CHUNKS, 2)


def exists(c, n=CHUNKS):
    return not isinstance(c, int) or 0 <= c < n


def walk(eng, step, n, behind):
    for c in range(UNROLL + 2):
        step(c, c, 0)
    with eng.Fori(1, n // UNROLL - 1) as i:
        for j in range(2, UNROLL + 2):
            step(UNROLL * i + j, j, i)
    for c in range(n - 2, n + behind):
        step(c, c % UNROLL, c // UNROLL)


def nodes_between(nc, a, K, acc, y_table, skip_table):
    WID = 2 * EMBED
    with ExitStack() as ctx:
        def sb(name, shape, dt=F32):
            return ctx.enter_context(nc.sbuf_tensor(name, shape, dt))

        def sem(name):
            return ctx.enter_context(nc.semaphore(name))

        x_sb = sb("x1_sb", [P, NODE_TILES, EMBED])
        w_sb = sb("w1_sb", [P, 2, WID])
        wo = sb("wo", [P, AGG0, EMBED])
        bo = sb("bo", [P, EMBED])
        nv = sb("nv", [P, NODE_TILES])
        mean_v = sb("mean_v", [P, 2, AGG0, P])
        y_sb = sb("y_sb", [P, 2, EMBED])
        N = NodePass(nc, ctx, "mid", K, x_sb, w_sb, WID)
        ps_r = N.ps_m
        ps_o = N.ps_t
        PIECES = 5
        n = NODE_TILES // PIECES
        s_x = [sem(f"m_x{q}") for q in range(PIECES)]
        places = WindowPlaces(nc, ctx, a, K, "mid", sem("m_places_in"), sem("m_places"))
        s_w, s_y, s_biased, s_scaled, s_recip = (
            sem(n) for n in ("m_w", "m_y", "m_biased", "m_scaled", "m_recip"))
        s_spread, s_mean, s_out, s_added, s_res, s_bias = (
            sem(n) for n in ("m_spread", "m_mean", "m_out", "m_added", "m_res", "m_bias"))
        s_stored = [sem(f"m_stored{i}") for i in range(2)]
        block = ctx.enter_context(nc.Block())
        h = NODE_TILES // 2

        @block.sync
        def _(sp):
            for dst, src in ((w_sb[:, :, :], a["wys"]), (wo[:, :, :], a["wo"]), (nv[:, :], a["nv"]),
                             (bo[:, :], a["bo"].to_broadcast([P, EMBED]))):
                sp.dma_start(dst, src).then_inc(s_w, 16)
            places.load(sp)
            for q in range(PIECES):
                sp.dma_start(x_sb[:, q * n:(q + 1) * n, :],
                             a["x"].rearrange("(i p) f -> p i f", p=P)[:, q * n:(q + 1) * n, :]).then_inc(s_x[q], 16)
            def both(i):
                for s in range(2):
                    sp.wait_ge(N.s_taken[s], i + 1)
                    sp.dma_start(y_table[bass.ds((2 * i + s) * P, P), :], y_sb[:, s, :]).then_inc(s_stored[s], 16)
                    sp.dma_start(skip_table[bass.ds((2 * i + s) * P, P), :],
                                 x_sb[:, bass.ds(2 * i + s, 1), :].rearrange("p a f -> p (a f)")
                                 ).then_inc(s_stored[s], 16)

            rounds(sp, h, both)
            for s in range(2):
                sp.wait_ge(s_stored[s], 32 * h)

        @block.vector
        def _(v):
            step = Count(v, N.s_step)
            v.wait_ge(s_w, 64)
            step(v.tensor_scalar(w_sb[:, :, 0:EMBED], w_sb[:, :, 0:EMBED], MUL ** -0.5, None, ALU.mult))
            step(v.tensor_scalar(w_sb[:, :, EMBED:WID], w_sb[:, :, EMBED:WID],
                                 math.sin(math.pi / 8.0) * MUL ** -0.5, None, ALU.mult))
            v.sem_inc(s_scaled, 1)

            places.work_out(v, CONV_TILES)

            def invert(j):
                v.reciprocal(acc[0:HEADS, 0, bass.ds(j * P, P)], acc[0:HEADS, 0, bass.ds(j * P, P)]).then_inc(s_recip, 1)

            def normalise(j, s):
                v.wait_ge(s_spread, j + 1)
                v.tensor_tensor(mean_v[:, s, :, :], acc[:, :, bass.ds(j * P, P)],
                                ps_r[s][:, 0:AGG0 * P].rearrange("p (k n) -> p k n", n=P),
                                ALU.mult).then_inc(s_mean, 1)

            def add(j, s):
                row = x_sb[:, bass.ds(j, 1), :].rearrange("p a f -> p (a f)")
                v.wait_ge(s_out, j + 1)
                v.tensor_tensor(row, row, ps_o[s][:, :, :].rearrange("p a b -> p (a b)"), ALU.add).then_inc(s_added, 1)

            def stats(j):
                v.wait_ge(s_added, j + 1)
                N.row_stats(v, j)

            def attend(j, s):
                if exists(j + 2, NODE_TILES):
                    invert(j + 2)
                normalise(j + 1, 1 - s)
                add(j, s)
                if exists(j - 1, NODE_TILES):
                    stats(j - 1)

            invert(0)
            invert(1)
            normalise(0, 0)
            v.wait_ge(s_biased, 1)
            attend(0, 0)
            for q in range(PIECES):
                v.wait_ge(s_biased, q + 1)
                with v.Fori(max(q * n // 2 - 1, 0), min((q + 1) * n // 2 - 1, h - 2)) as i:
                    attend(2 * i + 1, 1)
                    attend(2 * i + 2, 0)
            attend(NODE_TILES - 3, 1)
            attend(NODE_TILES - 2, 0)
            add(NODE_TILES - 1, 1)
            stats(NODE_TILES - 2)
            stats(NODE_TILES - 1)
            N.statistics(v, step)
            def both(i):
                for s in range(2):
                    j = 2 * i + s
                    row = x_sb[:, bass.ds(j, 1), :].rearrange("p a f -> p (a f)")
                    v.wait_ge(N.s_prod[s], i + 1)
                    v.wait_ge(s_stored[s], 32 * i)
                    v.tensor_scalar(y_sb[:, s, :], N.ps_m[s][:, 0:EMBED], nv[:, bass.ds(j, 1)], None,
                                    ALU.mult).then_inc(s_y, 1)
                    v.wait_ge(s_y, j + 1)
                    v.scalar_tensor_tensor(out=row, in0=N.ps_m[s][:, EMBED:WID], scalar=nv[:, bass.ds(j, 1)],
                                           in1=row, op0=ALU.mult, op1=ALU.add).then_inc(N.s_taken[s], 1)

            rounds(v, h, both)

        @block.gpsimd
        def _(gp):
            gp.wait_ge(s_w, 64)
            for q in range(PIECES):
                gp.wait_ge(s_x[q], 16)
                x = x_sb[:, q * n:(q + 1) * n, :]
                gp.tensor_tensor(x, x, bo[:, :].unsqueeze(1).to_broadcast([P, n, EMBED]), ALU.add).then_inc(s_biased, 1)

        @block.scalar
        def _(act):
            N.scalar(act)

        @block.tensor
        def _(pe):
            pe.wait_ge(s_w, 64)
            pe.wait_ge(s_scaled, 1)

            def spread(j, s):
                wait_then(pe, s_recip, j + 1, K.turn_pe)
                for k in range(AGG0):
                    mm = pe.matmul(ps_r[s][:, k * P:(k + 1) * P], K.place[:, k, :],
                                   acc[:, 0, bass.ds(j * P, P)], start=True, stop=True)
                mm.then_inc(s_spread, 1)

            def out(j, s):
                pe.wait_ge(s_mean, j + 1)
                for k in range(AGG0):
                    mm = pe.matmul(ps_o[s][:, :, :].rearrange("p a b -> p (a b)"), mean_v[:, s, k, :], wo[:, k, :],
                                   start=k == 0, stop=k == AGG0 - 1)
                mm.then_inc(s_out, 1)

            spread(0, 0)
            spread(1, 1)
            out(0, 0)
            def both(i):
                for s in range(2):
                    j = 2 * i + s + 1
                    pe.wait_ge(s_mean, j)
                    spread(j + 1, s)
                    pe.wait_ge(s_added, j - 1)
                    out(j, 1 - s)

            rounds(pe, h - 1, both)
            pe.wait_ge(s_added, NODE_TILES - 2)
            out(NODE_TILES - 1, 1)
            N.tensor(pe)


class ConvolutionSignals:

    def __init__(self, nc, ctx):
        def sem(*names):
            return [ctx.enter_context(nc.semaphore("c_" + n)) for n in names]

        self.idx, self.y, self.es = sem("idx0", "idx1"), sem("y0", "y1", "y2", "y3"), sem("es0", "es1", "es2", "es3")
        self.zero, self.blank = sem("zero", "blank")
        self.inputs, self.weights, self.hid, self.silu = sem("inputs", "weights", "hid", "silu")
        self.w, self.ad, self.far, self.sel, self.ax = sem("w", "ad", "far", "sel", "ax")
        self.dot, self.msg, self.agg, self.sum = sem("dot", "msg", "agg", "sum")


def convolution_edges(nc, a, K, acc, y_table, s_turn, S, wide):
    TS = CONV_TILES
    W = MUL if wide else CONV_NODES
    H = 2 if wide else 1
    WINDOWS = [(t, t + 1, h) for t in range(TS) for h in range(2)] if wide else [(0, TS, 0)]
    NW = len(WINDOWS)
    SLOTS = 1 if wide else 2
    STEPS = EDGE_TILES // TS
    U = UNROLL
    turn_pool, turn_pe = s_turn
    with ExitStack() as ctx:
        def sb(name, shape, dt=F32):
            return ctx.enter_context(nc.sbuf_tensor(f"{name}_c{H}", shape, dt))

        def psum(name, shape):
            return ctx.enter_context(nc.psum_tensor(f"{name}_c{H}", shape, F32))

        y = sb("y", [P, U, TS, EMBED])
        idx = sb("idx", [P, 2, TILES], I32)
        es = sb("es", [P, U, 2 * P])
        ea = sb("ea", [P, EDGE_TILES, 4])
        fc1 = sb("fc1", [P, P])
        fc2 = sb("fc2", [P, 2, EMBED])
        hid = sb("hid", [P, 2, 2 * P])
        w_ad = sb("w_ad", [P, 2, TS, P])
        y1e = sb("y1e", [P, TS, 3, MUL])
        dot = sb("dot", [P, TS, MUL])
        msg = sb("msg", [P, 2, TS, 3 * P])
        sel = sb("sel", [P, SLOTS, TS, H, 4, W])
        ps_h = [psum(f"ps_h{u}", [P, 512]) for u in range(2)]
        ps_ad = [psum(f"ps_ad{u}", [P, TS, P]) for u in range(2)]
        ps_cb = [psum(f"ps_cb{u}", [P, TS, P]) for u in range(2)]
        ps_a = [psum(f"ps_c{u}", [P, 512]) for u in range(2)]
        block = ctx.enter_context(nc.Block())

        @block.sync
        def _(sp):
            for dst, src in ((ea[:, :, :], a["ea"]), (fc1[:, :], a["fc1"]), (fc2[:, :, :], a["fc2"])):
                sp.dma_start(dst, src).then_inc(S.inputs, 16)

            def load(i):
                for m in range(U):
                    r = m // 2
                    if m % 2 == 0:
                        for k in range(2):
                            sp.wait_ge(S.y[m + k], i * 16 * TS)
                        sp.dma_start(idx[:, r, :],
                                     a["src_line"][bass.ds(2 * i + r, 1), :, :].rearrange("a p t -> p (a t)")
                                     ).then_inc(S.idx[r], 16)
                    if not isinstance(i, int):
                        sp.wait_ge(S.hid, U * i + m - U + 1)
                    sp.dma_start(es[0:2 * SCALARS, m, :], a["es"][bass.ds(U * i + m, 1), :, :].rearrange("a k n -> k (a n)")
                                 ).then_inc(S.es[m], 16)

            sp.wait_ge(S.blank, 1)
            load(0)
            with sp.Fori(1, STEPS // U) as i:
                load(i)

        @block.gpsimd
        def _(gp):
            def gather(i):
                for m in range(U):
                    if m % 2 == 0:
                        wait_then(gp, S.idx[m // 2], 16 * (i + 1), turn_pool)
                    if not isinstance(i, int):
                        wait_then(gp, S.msg, U * i + m - U + 1, turn_pool)
                    for t in range(TS):
                        q = (m % 2) * TS + t
                        gp.indirect_dma_start(y[:, m, t, :], None, y_table,
                                              bass.IndirectOffsetOnAxis(ap=idx[:, m // 2, q:q + 1].bitcast(U32), axis=0)
                                              ).then_inc(S.y[m], 16)

            gather(0)
            with gp.Fori(1, STEPS // U) as i:
                gather(i)

        @block.vector
        def _(v):
            v.memset(acc[:, 0:2, :], 0.0).then_inc(S.zero, 1)
            v.wait_ge(S.inputs, 48)
            v.tensor_scalar(fc2[:, :, :], fc2[:, :, :], 1.679 * MUL ** -0.5, None, ALU.mult).then_inc(S.weights, 1)
            v.wait_ge(S.zero, 1)
            v.wait_ge(S.blank, 4)

            def messages(g, r, i):
                u = r % 2
                y0 = y[:, r, :, 0:MUL]
                y1 = y[:, r, :, MUL:EMBED].rearrange("p t (c f) -> p t c f", c=3)
                axes = ea[:, bass.ds(g * TS, TS), 1:4].unsqueeze(3)
                v.wait_ge(S.y[r], 16 * TS * (i + 1))
                v.tensor_tensor(y1e[:, :, :, :], y1, axes.to_broadcast([P, TS, 3, MUL]), ALU.mult).then_inc(S.dot, 1)
                v.wait_ge(S.sel, g + 1)
                for h in range(H):
                    at = sel[:, u % SLOTS, :, h, :, :]
                    v.tensor_tensor(at[:, :, 1:4, :], at[:, :, 0:1, :].to_broadcast([P, TS, 3, W]),
                                    axes.to_broadcast([P, TS, 3, W]), ALU.mult).then_inc(S.ax, 1)
                v.wait_ge(S.dot, 3 * g + 1)
                v.tensor_tensor(dot[:, :, :], y1e[:, :, 0, :], y1e[:, :, 1, :], ALU.add).then_inc(S.dot, 1)
                v.wait_ge(S.w, g + 1)
                v.tensor_tensor(msg[:, u, :, EMBED + MUL:EMBED + P], ps_cb[u][:, :, 0:MUL], y0, ALU.mult)
                v.wait_ge(S.dot, 3 * g + 2)
                v.tensor_tensor(dot[:, :, :], dot[:, :, :], y1e[:, :, 2, :], ALU.add).then_inc(S.dot, 1)
                v.wait_ge(S.ad, g + 1)
                v.tensor_tensor(msg[:, u, :, 0:MUL], w_ad[:, u, :, 0:MUL], y0, ALU.mult)
                v.wait_ge(S.dot, 3 * g + 3)
                v.tensor_tensor(msg[:, u, :, EMBED:EMBED + MUL], ps_cb[u][:, :, MUL:P], dot[:, :, :], ALU.mult)
                v.tensor_tensor(msg[:, u, :, MUL:EMBED].rearrange("p t (c f) -> p t c f", c=3),
                                w_ad[:, u, :, MUL:P].unsqueeze(2).to_broadcast([P, TS, 3, MUL]), y1,
                                ALU.mult).then_inc(S.msg, 1)

            def add(g, u):
                for n, (t, _, h) in enumerate(WINDOWS):
                    n0 = v.value_load(K.first[0:1, bass.ds(g * TS + t, 1)], min_val=0, max_val=N_NODES)
                    nodes, ps = bass.ds(n0 + h * W if h else n0, W), ps_a[(u * NW + n) % 2]
                    v.wait_ge(S.agg, NW * g + n + 1)
                    v.wait_ge(S.sum, 3 * (NW * g + n))
                    v.tensor_tensor(acc[:, 0:2, nodes], acc[:, 0:2, nodes],
                                    ps[:, 4 * W:6 * W].rearrange("p (k w) -> p k w", w=W), ALU.add).then_inc(S.sum, 1)
                    v.tensor_tensor(acc[MUL:P, 2:5, nodes], acc[MUL:P, 2:5, nodes],
                                    ps[MUL:P, W:4 * W].rearrange("p (k w) -> p k w", w=W), ALU.add).then_inc(S.sum, 1)
                    v.tensor_tensor(acc[0:MUL, 2, nodes], acc[0:MUL, 2, nodes], ps[0:MUL, 0:W],
                                    ALU.add).then_inc(S.sum, 1)

            def step(g, j, i):
                if wide and exists(g - 1, STEPS):
                    add(g - 1, (j - 1) % 2)
                if exists(g, STEPS):
                    messages(g, j % U, i + j // U)
                if not wide and exists(g - 1, STEPS):
                    add(g - 1, (j - 1) % 2)

            walk(v, step, STEPS, 1)

        @block.scalar
        def _(act):
            def silu(g, u):
                act.wait_ge(S.hid, g + 1)
                act.activation(hid[:, u, :], ps_h[u][:, 0:2 * P], ACT.Silu, scale=SCALARS ** -0.5).then_inc(S.silu, 1)

            def select(g, u):
                if exists(g - SLOTS, STEPS):
                    act.wait_ge(S.agg, NW * (g - SLOTS + 1))
                at = sel[:, u % SLOTS, :, :, 0, :]
                for t in range(TS):
                    for h in range(H):
                        ins = act.activation(at[:, t, h, :], K.iota[:, h * W:(h + 1) * W], ACT.Square, scale=-1.0,
                                             bias=K.dst_rel[:, bass.ds(g * TS + t, 1)])
                ins.then_inc(S.far, 1)
                act.wait_ge(S.far, g + 1)
                act.activation(at, at, ACT.Relu, scale=-1.0, bias=1.0).then_inc(S.sel, 1)

            def step(g, j, i):
                if exists(g + 1, STEPS):
                    silu(g + 1, (j + 1) % 2)
                if exists(g, STEPS):
                    u = j % 2
                    act.wait_ge(S.w, g + 1)
                    for t in range(TS):
                        ins = act.activation(w_ad[:, u, t, :], ps_ad[u][:, t, :], ACT.Copy,
                                             scale=ea[:, bass.ds(g * TS + t, 1), 0:1].rearrange("p a b -> p (a b)"))
                    ins.then_inc(S.ad, 1)
                if exists(g + 1, STEPS):
                    select(g + 1, (j + 1) % 2)

            act.activation(es[:, :, :], K.ident[:, 0:1].unsqueeze(2).to_broadcast([P, U, 2 * P]), ACT.Copy,
                           scale=0.0).then_inc(S.blank, 1)
            for k in range(2, AGG1):
                act.activation(acc[:, k, :], K.ident[:, 0:1].to_broadcast([P, N_PAD]), ACT.Copy,
                               scale=0.0).then_inc(S.blank, 1)
            act.wait_ge(S.inputs, 48)
            silu(0, 0)
            select(0, 0)
            walk(act, step, STEPS, 0)

        @block.tensor
        def _(pe):
            def hidden(g, r, i):
                wait_then(pe, S.es[r], 16 * (i + 1), turn_pe)
                pe.matmul(ps_h[r % 2][:, 0:2 * P], fc1[:, :], es[:, r, :], start=True, stop=True).then_inc(S.hid, 1)

            def weights(g, u):
                pe.wait_ge(S.silu, g + 1)
                if exists(g - 2, STEPS):
                    pe.wait_ge(S.msg, g - 1)
                for t in range(TS):
                    for q, out in enumerate((ps_ad[u], ps_cb[u])):
                        mm = pe.matmul(out[:, t, :], hid[:, u, (t % 2) * P:(t % 2 + 1) * P],
                                       fc2[:, t // 2, q * P:(q + 1) * P], start=True, stop=True)
                mm.then_inc(S.w, 1)

            def sums(g, u):
                pe.wait_ge(S.msg, g + 1)
                for n, (t0, t1, h) in enumerate(WINDOWS):
                    out = ps_a[(u * NW + n) % 2]
                    if exists(g - 1, STEPS) or n > 1:
                        pe.wait_ge(S.sum, 3 * (NW * g + n - 1))
                    for t in range(t0, t1):
                        at = sel[:, u % SLOTS, t, h, :, :]
                        pe.matmul(out[:, 0:4 * W], msg[:, u, t, 2 * P:3 * P], at.rearrange("p k w -> p (k w)"),
                                  start=t == t0, stop=t == t1 - 1, skip_group_check=True)
                        for m in range(2):
                            mm = pe.matmul(out[:, (4 + m) * W:(5 + m) * W], msg[:, u, t, m * P:(m + 1) * P],
                                           at[:, 0, :], start=False, stop=t == t1 - 1, skip_group_check=True)
                    mm.then_inc(S.agg, 1)

            def step(g, j, i):
                if exists(g + 1, STEPS):
                    hidden(g + 1, (j + 1) % U, i + (j + 1) // U)
                if exists(g, STEPS):
                    weights(g, j % 2)
                if exists(g - 1, STEPS):
                    sums(g - 1, (j - 1) % 2)

            pe.wait_ge(S.inputs, 48)
            pe.wait_ge(S.weights, 1)
            hidden(0, 0, 0)
            walk(pe, step, STEPS, 1)


def nodes_after(nc, a, K, acc, skip_table):
    with ExitStack() as ctx:
        def sb(name, shape, dt=F32):
            return ctx.enter_context(nc.sbuf_tensor(name, shape, dt))

        def sem(name):
            return ctx.enter_context(nc.semaphore(name))

        x_sb = sb("skip", [P, NODE_TILES, EMBED])
        OUT = AGG1 - 1
        w_sb = sb("w_fin", [P, OUT, EMBED])
        nv = sb("nv_fin", [P, NODE_TILES])
        own = sb("own", [P, 2, OUT, P])
        ps = [ctx.enter_context(nc.psum_tensor(f"ps_f{s}", [P, 512], F32)) for s in range(2)]
        s_w, s_scaled, s_own, s_out = (sem("f_" + n) for n in ("w", "scaled", "own", "out"))
        PIECES = 5
        n = NODE_TILES // PIECES
        s_x = [sem(f"f_x{q}") for q in range(PIECES)]
        s_fin = [sem(f"f_fin{s}") for s in range(2)]
        s_prod = [sem(f"f_prod{s}") for s in range(2)]
        block = ctx.enter_context(nc.Block())
        h = NODE_TILES // 2

        @block.sync
        def _(sp):
            sp.dma_start(w_sb[:, :, :], a["wfin"].rearrange("k p f -> p k f")).then_inc(s_w, 16)
            sp.dma_start(nv[:, :], a["nv"]).then_inc(s_w, 16)
            for q in range(PIECES):
                sp.dma_start(x_sb[:, q * n:(q + 1) * n, :],
                             skip_table.rearrange("(i p) f -> p i f", p=P)[:, q * n:(q + 1) * n, :]).then_inc(s_x[q], 16)
            def both(i):
                for s in range(2):
                    j = 2 * i + s
                    sp.wait_ge(s_fin[s], i + 1)
                    sp.dma_start(a["out"][bass.ds(j * P, P), :],
                                 x_sb[:, bass.ds(j, 1), :].rearrange("p a f -> p (a f)")).then_inc(s_out, 16)

            rounds(sp, h, both)
            sp.wait_ge(s_out, 16 * NODE_TILES)

        @block.vector
        def _(v):
            scale = math.cos(math.pi / 8.0) / math.sqrt(2 * MUL) / math.sqrt(20.0)
            v.wait_ge(s_w, 32)
            v.tensor_scalar(w_sb[:, 0:2, :], w_sb[:, 0:2, :], scale, None, ALU.mult).then_inc(s_scaled, 1)
            for q, m, f in ((slice(0, MUL), 2, scale / math.sqrt(3.0)), (slice(MUL, P), 2, scale), (slice(0, P), 3, scale)):
                v.tensor_scalar(w_sb[q, m, :], w_sb[q, m, :], f, None, ALU.mult).then_inc(s_scaled, 1)
            for q in range(PIECES):
                v.wait_ge(s_x[q], 16)
                with v.Fori(q * n // 2, (q + 1) * n // 2) as i:
                    for s in range(2):
                        j = 2 * i + s
                        row = x_sb[:, bass.ds(j, 1), :].rearrange("p a f -> p (a f)")
                        v.wait_ge(s_prod[s], i + 1)
                        v.scalar_tensor_tensor(out=row, in0=ps[s][:, 0:EMBED], scalar=nv[:, bass.ds(j, 1)], in1=row,
                                               op0=ALU.mult, op1=ALU.add).then_inc(s_fin[s], 1)

        @block.scalar
        def _(act):
            def both(i):
                for s in range(2):
                    act.wait_ge(s_prod[s], i)
                    nodes = bass.ds((2 * i + s) * P, P)
                    act.activation(own[:, s, 0:3, :], acc[:, 0:3, nodes], ACT.Copy).then_inc(s_own, 1)
                    act.activation(own[MUL:P, s, 3, :], acc[MUL:P, 3, nodes], ACT.Copy).then_inc(s_own, 1)
                    act.activation(own[0:MUL, s, 3, :], acc[MUL:P, 4, nodes], ACT.Copy).then_inc(s_own, 1)

            rounds(act, h, both)

        @block.tensor
        def _(pe):
            pe.wait_ge(s_scaled, 4)
            def both(i):
                for s in range(2):
                    pe.wait_ge(s_own, 3 * (2 * i + s + 1))
                    pe.wait_ge(s_fin[s], i)
                    for k in range(OUT):
                        mm = pe.matmul(ps[s][:, 0:EMBED], own[:, s, k, :], w_sb[:, k, :], start=k == 0, stop=k == OUT - 1)
                    mm.then_inc(s_prod[s], 1)

            rounds(pe, h, both)


def kernel(**inputs):
    import numpy as np
    import concourse.bacc as bacc
    from concourse.bass_utils import run_bass_kernel_spmd

    d = {k: np.asarray(x) for k, x in inputs.items()}
    f = np.float32

    def rows(x, n, value=0):
        return np.concatenate([x, np.full((n - x.shape[0],) + x.shape[1:], value, x.dtype)])

    def by_tile(x):
        return np.ascontiguousarray(np.swapaxes(x.reshape(EDGE_TILES, P, *x.shape[1:]), 0, 1))

    src = rows(d["src"].astype(np.int32), E_PAD)
    dst = rows(d["dst"].astype(np.int32), E_PAD, N_NODES)
    ext = np.concatenate([np.full(1, -1, np.int32), dst])
    es = rows(d["edge_attr_8"], E_PAD).reshape(EDGE_TILES // 4, 2, 2, P, SCALARS)
    es = es.transpose(0, 1, 4, 2, 3).reshape(EDGE_TILES // 4, 2 * SCALARS, 2 * P)
    L0 = {n: d["L0_gnn_" + n] for n in ("Wq", "bq", "Wk", "bk", "Wv", "bv", "Wo", "bo")}
    L1 = {n: d["L1_gnn_" + n] for n in ("sc_w0", "sc_w1", "lin1_w0", "lin1_w1", "fc_w1", "fc_w2",
                                        "lin2_w00", "lin2_w01", "lin2_w10", "lin2_w11")}
    wqkv = np.concatenate([L0["Wk"].T, L0["Wv"].T, L0["Wq"].T], 1).reshape(2, P, 3 * EMBED).transpose(1, 0, 2)
    wo = np.concatenate([np.zeros((HEADS, EMBED), f), L0["Wo"].T]).reshape(AGG0, ROWS, EMBED).transpose(1, 0, 2)
    wo = np.pad(wo, ((0, P - ROWS), (0, 0), (0, 0)))
    wys = np.zeros((EMBED, 2 * EMBED), f)
    wfin = np.zeros((AGG1 - 1, P, EMBED), f)
    wys[:MUL, :MUL] = L1["lin1_w0"]
    wys[:MUL, EMBED:EMBED + MUL] = L1["sc_w0"]
    wfin[0, :MUL, :MUL] = L1["lin2_w00"]
    wfin[2, :MUL, :MUL] = L1["lin2_w01"]
    for c in range(3):
        wys[MUL + c::3, MUL * (c + 1):MUL * (c + 2)] = L1["lin1_w1"]
        wys[MUL + c::3, EMBED + MUL + c::3] = L1["sc_w1"]
        wfin[(c + 1) // 2, ((c + 1) % 2) * MUL:((c + 1) % 2 + 1) * MUL, MUL + c::3] = L1["lin2_w11"]
        block, low = ((2, MUL), (3, MUL), (3, 0))[c]
        wfin[block, low:low + MUL, MUL + c::3] = L1["lin2_w10"]
    wys = wys.reshape(2, P, 2 * EMBED).transpose(1, 0, 2)
    fc1 = np.zeros((P, P), f)
    fc1[:SCALARS, :MUL] = fc1[SCALARS:2 * SCALARS, MUL:] = L1["fc_w1"]
    part = [L1["fc_w2"][:, MUL * k:MUL * (k + 1)] for k in (0, 3, 2, 1)]
    fc2 = np.zeros((P, 2, EMBED), f)
    fc2[:MUL, 0] = fc2[MUL:, 1] = np.concatenate(part, 1)
    place = np.zeros((P, AGG0 * ROWS), f)
    for h in range(HEADS):
        place[h, h] = 1.0
        place[h, HEADS + h * HDIM:HEADS + (h + 1) * HDIM] = 1.0
    arrays = {
        "x": rows(d["x"], N_PAD),
        "src_line": src.reshape(CHUNKS, TILES, P).transpose(0, 2, 1),
        "dst_tile": by_tile(dst),
        "dst_line": np.lib.stride_tricks.sliding_window_view(ext, CHUNK + 1)[::CHUNK],
        "first": dst[None, ::P],
        "last": dst[None, P - 1::P],
        "ident": np.eye(P, dtype=f),
        "iota": np.arange(P, dtype=f)[None],
        "part": np.arange(P, dtype=f)[:, None],
        "place": np.pad(place.reshape(P, AGG0, ROWS), ((0, 0), (0, 0), (0, P - ROWS))),
        "wqkv": wqkv, "bqkv": np.concatenate([L0["bk"], L0["bv"], L0["bq"]])[None],
        "wo": wo, "bo": L0["bo"][None], "wys": wys, "wfin": wfin, "fc1": fc1, "fc2": fc2,
        "nv": rows(d["node_vec1"], N_PAD)[:, 0].reshape(NODE_TILES, P).T,
        "ea": by_tile(rows(d["edge_attr_4"], E_PAD)),
        "es": es,
    }
    nc = bacc.Bacc("TRN2", target_bir_lowering=False, num_devices=1)
    aps, feed = {}, {}
    for n, x in arrays.items():
        x = np.ascontiguousarray(x)
        feed["in_" + n] = x
        aps[n] = nc.dram_tensor("in_" + n, x.shape, mybir.dt.from_np(x.dtype), kind="ExternalInput").ap()
    aps["out"] = nc.dram_tensor("out", (N_PAD, EMBED), F32, kind="ExternalOutput").ap()
    build(nc, aps)
    r = run_bass_kernel_spmd(nc, [feed], core_ids=[0])
    return r.results[0]["out"][:N_NODES]
```
